# Optimizing a Trainium2 kernel written in Bass

```python
import numpy as np
import jax
import jax.numpy as jnp

def _softmax(x, axis=-1):
    return jax.nn.softmax(x, axis=axis)

def _gelu(x):
    return jax.nn.gelu(x, approximate=True)

def _silu(x):
    return jax.nn.silu(x)

def _sigmoid(x):
    return jax.nn.sigmoid(x)

def _layernorm(x, axis=-1, eps=1e-05):
    m = jnp.mean(x, axis=axis, keepdims=True)
    v = jnp.var(x, axis=axis, keepdims=True)
    return (x - m) / jnp.sqrt(v + eps)

def _scatter_add(tgt, idx, src, axis=0):
    return tgt.at[idx].add(src)

def _segment_sum(src, seg, n):
    return jax.ops.segment_sum(src, seg, n)
kernel_name = 'mk_gnn_resnorm_d1_gnn_r64_013eec'

def setup_inputs(seed: int=0):
    np.random.seed(seed)
    _w = jnp.asarray

    def _rec_inputs():
        import jax
        import jax.numpy as jnp
        _gk = jax.random.key(seed)
        x = -0.0001006 + 1 * jax.random.normal(jax.random.fold_in(_gk, 1), (100000, 48), jnp.float32)
        src = jax.random.randint(jax.random.fold_in(_gk, 2), (25000,), 0, 100000, jnp.int32)
        dst = jax.random.randint(jax.random.fold_in(_gk, 3), (25000,), 0, 100000, jnp.int32)
        _o = jnp.argsort(dst, stable=True)
        src = src[_o]
        dst = dst[_o]
        edge_attr_32 = 0.000189758 + 1.00013 * jax.random.normal(jax.random.fold_in(_gk, 11), (25000, 32), jnp.float32)
        return (x, src, dst, edge_attr_32)
    x, src, dst, edge_attr_32 = _rec_inputs()

    def _L0_gnn_setup():
        import jax, jax.numpy as jnp
        import numpy as np
        N_NODES = 100000
        key = jax.random.key(seed)
        k1, k2, k3, k4, k5, k6 = jax.random.split(key, 6)
        node_dim, edge_dim, hidden = (48, 32, 128)
        E = 25000
        x = jax.random.normal(k1, (N_NODES, node_dim), dtype=jnp.float32)
        edge_index = jax.random.randint(k2, (2, E), 0, N_NODES, dtype=jnp.int64)
        edge_attr = jax.random.normal(k3, (E, edge_dim), dtype=jnp.float32)
        in_dim = 2 * node_dim + edge_dim
        s1 = 1.0 / np.sqrt(in_dim)
        s2 = 1.0 / np.sqrt(hidden)
        W1 = jax.random.uniform(k4, (in_dim, hidden), minval=-s1, maxval=s1, dtype=jnp.float32)
        b1 = jax.random.uniform(k5, (hidden,), minval=-s1, maxval=s1, dtype=jnp.float32)
        W2 = jax.random.uniform(k6, (hidden, node_dim), minval=-s2, maxval=s2, dtype=jnp.float32)
        b2 = jnp.zeros((node_dim,), dtype=jnp.float32)
        return {'x': x, 'edge_index': edge_index, 'edge_attr': edge_attr, 'W1': W1, 'b1': b1, 'W2': W2, 'b2': b2}
    _L0_gnn_all = _L0_gnn_setup()
    _L0_gnn_in = {k: v for k, v in _L0_gnn_all.items() if k in ('W1', 'b1', 'W2', 'b2')}
    del _L0_gnn_all
    return {'x': x, 'src': src, 'dst': dst, 'edge_attr_32': edge_attr_32, 'L0_gnn_W1': _L0_gnn_in['W1'], 'L0_gnn_b1': _L0_gnn_in['b1'], 'L0_gnn_W2': _L0_gnn_in['W2'], 'L0_gnn_b2': _L0_gnn_in['b2']}

def reference(x, src, dst, edge_attr_32, L0_gnn_W1, L0_gnn_b1, L0_gnn_W2, L0_gnn_b2):
    import jax
    import jax.numpy as jnp

    def _L0_gnn_ref(x, edge_index, edge_attr, W1, b1, W2, b2):
        import jax, jax.numpy as jnp
        import numpy as np
        N_NODES = 100000
        src, dst = (edge_index[0], edge_index[1])
        x_i = x[dst]
        x_j = x[src]
        tmp = jnp.concatenate([x_i, x_j, edge_attr], axis=1)
        h = jax.nn.relu(tmp @ W1 + b1)
        msg = h @ W2 + b2
        out = jax.ops.segment_sum(msg, dst, num_segments=N_NODES)
        return out
    edge_index = jnp.stack([src, dst])
    x = _layernorm(x + _L0_gnn_ref(x, edge_index, edge_attr_32, L0_gnn_W1, L0_gnn_b1, L0_gnn_W2, L0_gnn_b2), axis=-1)
    return x

_drawn_inputs = setup_inputs


def setup_inputs(seed=0):
    import zlib

    import numpy as np

    out = dict(_drawn_inputs(seed))
    spreads = {'L0_gnn_b2': (0.0, 0.1)}
    factors = {'L0_gnn_b1': 5.48}
    for name, (base, spread) in spreads.items():
        noise = np.random.default_rng([zlib.crc32(name.encode()), seed]).standard_normal(out[name].shape)
        drawn = base * np.exp(spread * noise) if base else spread * noise
        out[name] = jnp.asarray(drawn.astype(out[name].dtype))
    for name, factor in factors.items():
        out[name] = (out[name] * factor).astype(out[name].dtype)
    return out
```

```python
from contextlib import ExitStack

import concourse.bass as bass
from concourse import mybir

P = 128
F32 = mybir.dt.float32
I32 = mybir.dt.int32
ALU = mybir.AluOpType
ACT = mybir.ActivationFunctionType
AX_X = mybir.AxisListType.X
EPS = 1e-5

UNROLL = 5
SCATTER_LAG = 2
LN_SLOTS = 3


def gnn_resnorm_kernel(nc, x, src, dst, edge_attr, W1, b1, W2, b2, out):
    N, D = x.shape
    E, DE = edge_attr.shape
    FIN, HID = W1.shape
    assert FIN == P and HID == P and 2 * D + DE == P
    TILES = E // P
    TAIL = E - TILES * P
    ROUNDS = TILES // UNROLL
    assert ROUNDS * UNROLL == TILES and ROUNDS > 2 and TAIL > 0
    PER = N // P
    REST = N - PER * P
    CHUNKS = 11
    G = PER // CHUNKS
    assert G * CHUNKS == PER and REST > 0 and (N * D) % (3 * P) == 0

    acc = nc.dram_tensor("acc", (N + P, D), F32, kind="Internal").ap()

    with ExitStack() as ctx:
        def sb(name, shape, dt=F32):
            return ctx.enter_context(nc.sbuf_tensor(name, shape, dt))

        def ps(name, shape):
            return ctx.enter_context(nc.psum_tensor(name, shape, F32))

        def sem(name):
            return ctx.enter_context(nc.semaphore(name))

        src_idx = sb("src_idx", [P, TILES + 1], I32)
        dst_idx = sb("dst_idx", [P, TILES + 1], I32)
        node_idx = sb("node_idx", [P, TILES + UNROLL, 2], I32)
        tile_idx = sb("tile_idx", [P, UNROLL, 2], I32)
        dst_f = sb("dst_f", [P, TILES + 1])
        tile_dst = sb("tile_dst", [P, UNROLL])
        spare_less_dst = sb("spare_less_dst", [P, TILES + 1])
        spare_row_i = sb("spare_row_i", [P, 1], I32)
        spare_row = sb("spare_row", [P, 1])
        ident = sb("ident", [P, P])
        lower = sb("lower", [P, P])
        ones_row = sb("ones_row", [1, P])
        w1 = sb("w1", [P, HID])
        b1c = sb("b1c", [HID, 1])
        w2 = sb("w2", [HID, D])
        b2r = sb("b2r", [1, D])
        cat = sb("cat", [P, UNROLL, P])
        cat_t = sb("cat_t", [P, UNROLL, P])
        hid_t = sb("hid_t", [P, UNROLL, P])
        msg = sb("msg", [P, UNROLL, D])
        same = sb("same", [P, UNROLL, P])
        earlier = sb("earlier", [P, UNROLL, P])
        n_earlier = sb("n_earlier", [P, UNROLL])
        repeated = sb("repeated", [P, UNROLL])
        row_idx = sb("row_idx", [P, UNROLL, 1], I32)
        sums = sb("sums", [P, UNROLL, D])
        bank = [ps(f"bank{u}", [P, 512]) for u in range(UNROLL)]
        cat_ps = [b[:, 0:P] for b in bank]
        hid_ps = [b[:, P:2 * P] for b in bank]
        dst_ps = [b[:, 2 * P:3 * P] for b in bank]
        msg_ps = [b[:, 3 * P:3 * P + D] for b in bank]
        sum_ps = [b[:, 3 * P + 64:3 * P + 64 + D] for b in bank]
        xa = sb("xa", [P, LN_SLOTS, G, D])
        xsq = sb("xsq", [P, LN_SLOTS, G, D])
        mean = sb("mean", [P, LN_SLOTS, G])
        var = sb("var", [P, LN_SLOTS, G])
        std = sb("std", [P, LN_SLOTS, G])
        rstd = sb("rstd", [P, LN_SLOTS, G])
        eps = sb("eps", [P, 1])

        idx_in = sem("idx_in")
        weights_in = sem("weights_in")
        acc_start = sem("acc_start")
        consts = sem("consts")
        const_base = sem("const_base")
        dst_ready = sem("dst_ready")
        dst_placed = sem("dst_placed")
        may_gather = sem("may_gather")
        may_scatter = sem("may_scatter")
        idx_base = sem("idx_base")
        idx_paired = sem("idx_paired")
        idx_placed = sem("idx_placed")
        edge_in = [sem(f"edge_in{u}") for u in range(UNROLL)]
        xdst_in = [sem(f"xdst_in{u}") for u in range(UNROLL)]
        xsrc_in = [sem(f"xsrc_in{u}") for u in range(UNROLL)]
        cat_placed = sem("cat_placed")
        cat_copied = sem("cat_copied")
        hid_done = sem("hid_done")
        relu_done = sem("relu_done")
        msg_done = sem("msg_done")
        msg_copied = sem("msg_copied")
        dst_spread = sem("dst_spread")
        same_done = sem("same_done")
        step_done = sem("step_done")
        row_done = sem("row_done")
        sum_done = sem("sum_done")
        sum_copied = sem("sum_copied")
        scattered = sem("scattered")
        chunk_in = [sem(f"chunk_in{s}") for s in range(LN_SLOTS)]
        mean_done = sem("mean_done")
        centred = sem("centred")
        squared = sem("squared")
        var_done = sem("var_done")
        std_done = sem("std_done")
        rstd_done = sem("rstd_done")
        normed = sem("normed")
        ln_step = sem("ln_step")
        chunk_out = [sem(f"chunk_out{s}") for s in range(LN_SLOTS)]

        main = TILES * P
        src_v = src[0:main].rearrange("(p t) -> p t", p=P)
        dst_v = dst[0:main].rearrange("(p t) -> p t", p=P)
        edge_v = edge_attr[0:main, :].rearrange("(p t) d -> p t d", p=P)

        def rows(t):
            return TAIL if isinstance(t, int) and t == TILES else P

        def tiles(eng, step):
            for u in range(UNROLL):
                step(0, u)
            with eng.Fori(1, ROUNDS) as r:
                for u in range(UNROLL):
                    step(r, u)
            step(ROUNDS, 0)

        def tile_of(r, u):
            return r * UNROLL + u

        def ln_rows(c):
            return P if c < CHUNKS else REST

        def ln_cols(c):
            return G if c < CHUNKS else 1

        def ln_pair(c, table, tile):
            s = c % LN_SLOTS
            if c < CHUNKS:
                t = table[0:PER * P, :].rearrange("(p j) d -> p j d", p=P)[:, c * G:(c + 1) * G, :]
                return t, tile[:, s, :, :]
            return table[PER * P:N, :], tile[0:REST, s, 0, :]

        block = ctx.enter_context(nc.Block())

        @block.sync
        def _(sp):
            sp.dma_start(dst_idx[:, 0:TILES], dst_v).then_inc(idx_in, 16)
            sp.dma_start(src_idx[:, 0:TILES], src_v).then_inc(idx_in, 16)
            sp.dma_start(dst_idx[0:TAIL, TILES:TILES + 1], dst[main:E].rearrange("(p t) -> p t", t=1)).then_inc(idx_in, 16)
            sp.dma_start(src_idx[0:TAIL, TILES:TILES + 1], src[main:E].rearrange("(p t) -> p t", t=1)).then_inc(idx_in, 16)
            sp.dma_start(w1[:, :], W1).then_inc(weights_in, 16)
            sp.dma_start(w2[:, :], W2).then_inc(weights_in, 16)
            sp.dma_start(b1c[:, :], b1.rearrange("(p t) -> p t", t=1)).then_inc(weights_in, 16)
            sp.dma_start(b2r[:, :], b2.rearrange("(a d) -> a d", a=1)).then_inc(weights_in, 16)

            def load_edges(r, u):
                t = tile_of(r, u)
                n = rows(t)
                if not (isinstance(r, int) and r == 0):
                    sp.wait_ge(cat_placed, t - UNROLL + 1)
                source = edge_attr[main:E, :] if n == TAIL else edge_v[:, bass.ds(t, 1), :].rearrange("p t d -> p (t d)")
                sp.dma_start(cat[0:n, u, 2 * D:P], source).then_inc(edge_in[u], 16)

            tiles(sp, load_edges)
            sp.wait_ge(scattered, 16 * (TILES + 1))
            for c in range(CHUNKS + 1):
                s = c % LN_SLOTS
                if c >= LN_SLOTS:
                    sp.wait_ge(chunk_out[s], 16 * (c // LN_SLOTS))
                sp.dma_start(*ln_pair(c, acc, xa)[::-1]).then_inc(chunk_in[s], 16)

        @block.gpsimd
        def _(pool):
            pool.memset(ident[:, :], 0.0).then_inc(const_base, 1)
            pool.memset(lower[:, :], 1.0).then_inc(const_base, 1)
            pool.wait_ge(const_base, 2)
            pool.affine_select(out=ident[:, :], in_=ident[:, :], pattern=[[-1, P]], compare_op=ALU.not_equal,
                               fill=1.0, base=0, channel_multiplier=1).then_inc(consts, 1)
            pool.affine_select(out=lower[:, :], in_=lower[:, :], pattern=[[-1, P]], compare_op=ALU.is_gt,
                               fill=0.0, base=0, channel_multiplier=1).then_inc(consts, 1)
            pool.iota(spare_row_i[:, :], pattern=[[0, 1]], base=N, channel_multiplier=1).then_inc(consts, 1)

            def gather(r, u):
                t = tile_of(r, u)
                n = rows(t)
                if not (isinstance(r, int) and r == 0):
                    pool.wait_ge(cat_placed, t - UNROLL + 1)
                pool.wait_ge(idx_placed, t + 1)
                pool.sem_inc(may_gather, 1)
                pool.indirect_dma_start(cat[0:n, u, 0:D], None, x[:, :],
                                        bass.IndirectOffsetOnAxis(ap=tile_idx[0:n, u, 0:1], axis=0)).then_inc(xdst_in[u], 16)
                pool.indirect_dma_start(cat[0:n, u, D:2 * D], None, x[:, :],
                                        bass.IndirectOffsetOnAxis(ap=tile_idx[0:n, u, 1:2], axis=0)).then_inc(xsrc_in[u], 16)

            def scatter(t, u):
                n = rows(t)
                pool.wait_ge(sum_copied, t + 1)
                pool.wait_ge(row_done, t + 1)
                if not (isinstance(t, int) and t == 0):
                    pool.wait_ge(scattered, 16 * t)
                pool.sem_inc(may_scatter, 1)
                pool.indirect_dma_start(acc[:, :], bass.IndirectOffsetOnAxis(ap=row_idx[0:n, u, :], axis=0),
                                        sums[0:n, u, :], None, compute_op=ALU.add).then_inc(scattered, 16)

            for u in range(UNROLL):
                gather(0, u)
                if u == SCATTER_LAG:
                    pool.wait_ge(acc_start, 32)
                if u >= SCATTER_LAG:
                    scatter(u - SCATTER_LAG, u - SCATTER_LAG)
            with pool.Fori(1, ROUNDS) as r:
                for u in range(UNROLL):
                    gather(r, u)
                    scatter(tile_of(r, u) - SCATTER_LAG, (u - SCATTER_LAG) % UNROLL)
            gather(ROUNDS, 0)
            for t in range(TILES - SCATTER_LAG, TILES + 1):
                scatter(t, t % UNROLL)
            for c in range(CHUNKS + 1):
                s, n, g = c % LN_SLOTS, ln_rows(c), ln_cols(c)
                pool.wait_ge(rstd_done, c + 1)
                pool.tensor_tensor(xa[0:n, s, 0:g, :], xa[0:n, s, 0:g, :],
                                   rstd[0:n, s, 0:g].unsqueeze(2).broadcast_to([n, g, D]), ALU.mult).then_inc(normed, 1)

        @block.tensor
        def _(pe):
            pe.wait_ge(consts, 2)
            pe.wait_ge(weights_in, 64)
            pe.wait_ge(dst_ready, 2)

            def step(r, u):
                t = tile_of(r, u)
                n = rows(t)
                first = isinstance(r, int) and r == 0
                if not first:
                    pe.wait_ge(sum_copied, t - UNROLL + 1)
                pe.wait_ge(dst_placed, t + 1)
                pe.transpose(dst_ps[u][0:n, 0:n], tile_dst[0:n, u:u + 1].broadcast_to([n, n]),
                             ident[0:n, 0:n]).then_inc(dst_spread, 1)
                rr = 16 * (r + 1)
                pe.wait_ge(edge_in[u], rr)
                pe.wait_ge(xdst_in[u], rr)
                pe.wait_ge(xsrc_in[u], rr)
                pe.wait_ge(same_done, t + 1)
                pe.transpose(cat_ps[u][:, 0:n], cat[0:n, u, :], ident[0:n, 0:n]).then_inc(cat_placed, 1)
                pe.wait_ge(cat_copied, t + 1)
                pe.matmul(hid_ps[u][:, 0:n], w1[:, :], cat_t[:, u, 0:n], start=True, stop=True).then_inc(hid_done, 1)
                pe.wait_ge(relu_done, t + 1)
                pe.matmul(msg_ps[u][0:n, :], hid_t[:, u, 0:n], w2[:, :], start=True, stop=False)
                pe.matmul(msg_ps[u][0:n, :], ones_row[0:1, 0:n], b2r[:, :], start=False, stop=True).then_inc(msg_done, 1)
                pe.wait_ge(msg_copied, t + 1)
                pe.matmul(sum_ps[u][0:n, :], same[0:n, u, 0:n], msg[0:n, u, :], start=True, stop=True).then_inc(sum_done, 1)

            tiles(pe, step)

        @block.scalar
        def _(act):
            flat_x = x.rearrange("n d -> (n d)").rearrange("(k m) -> k m", k=3 * P)
            flat_a = acc[0:N, :].rearrange("n d -> (n d)").rearrange("(k m) -> k m", k=3 * P)
            act.dma_start(flat_a, flat_x).then_inc(acc_start, 16)
            act.dma_start(acc[N:N + P, :], x[0:P, :]).then_inc(acc_start, 16)
            act.wait_ge(idx_paired, 4)
            for t in range(UNROLL - 1):
                act.activation(tile_idx[:, t, :], node_idx[:, t, :], ACT.Copy).then_inc(idx_placed, 1)
            act.wait_ge(weights_in, 64)

            def step(r, u):
                t = tile_of(r, u)
                n = rows(t)
                act.wait_ge(cat_placed, t + 1)
                act.activation(cat_t[:, u, 0:n], cat_ps[u][:, 0:n], ACT.Copy).then_inc(cat_copied, 1)
                if not (isinstance(r, int) and r == ROUNDS):
                    act.activation(tile_idx[:, (u - 1) % UNROLL, :],
                                   node_idx[:, bass.ds(t + UNROLL - 1, 1), :].rearrange("p t k -> p (t k)"),
                                   ACT.Copy).then_inc(idx_placed, 1)
                act.wait_ge(hid_done, t + 1)
                act.activation(hid_t[:, u, 0:n], hid_ps[u][:, 0:n], ACT.Relu, bias=b1c[:, 0:1]).then_inc(relu_done, 1)

            tiles(act, step)
            for c in range(CHUNKS + 2):
                if c <= CHUNKS:
                    s, n, g = c % LN_SLOTS, ln_rows(c), ln_cols(c)
                    act.wait_ge(centred, c + 1)
                    if c >= LN_SLOTS:
                        act.wait_ge(var_done, c - LN_SLOTS + 1)
                    act.activation(xsq[0:n, s, 0:g, :], xa[0:n, s, 0:g, :], ACT.Square).then_inc(squared, 1)
                    act.wait_ge(var_done, c + 1)
                    act.activation(std[0:n, s, 0:g], var[0:n, s, 0:g], ACT.Sqrt, bias=eps[0:n, 0:1],
                                   scale=1.0 / D).then_inc(std_done, 1)
                if c >= 1:
                    act.wait_ge(normed, c)
                    act.dma_start(*ln_pair(c - 1, out, xa)).then_inc(chunk_out[(c - 1) % LN_SLOTS], 16)
            for s in range(LN_SLOTS):
                act.wait_ge(chunk_out[s], 16 * len(range(s, CHUNKS + 1, LN_SLOTS)))

        @block.vector
        def _(dve):
            dve.memset(eps[:, :], EPS).then_inc(dst_ready, 1)
            dve.memset(ones_row[:, :], 1.0).then_inc(dst_ready, 1)
            dve.memset(node_idx[:, TILES:TILES + UNROLL, :], 0).then_inc(idx_base, 1)
            dve.wait_ge(idx_in, 64)
            dve.wait_ge(idx_base, 1)
            for k, idx in enumerate((dst_idx, src_idx)):
                dve.tensor_copy(node_idx[:, 0:TILES, k], idx[:, 0:TILES]).then_inc(idx_paired, 1)
                dve.tensor_copy(node_idx[0:TAIL, TILES, k:k + 1], idx[0:TAIL, TILES:TILES + 1]).then_inc(idx_paired, 1)
            dve.wait_ge(consts, 3)
            dve.tensor_copy(spare_row[:, :], spare_row_i[:, :]).then_inc(dst_ready, 1)
            dve.tensor_copy(dst_f[:, 0:TILES], dst_idx[:, 0:TILES]).then_inc(dst_ready, 1)
            dve.tensor_copy(dst_f[0:TAIL, TILES:TILES + 1], dst_idx[0:TAIL, TILES:TILES + 1]).then_inc(dst_ready, 1)
            dve.wait_ge(dst_ready, 5)
            dve.tensor_scalar(spare_less_dst[:, 0:TILES], dst_f[:, 0:TILES], -1.0, spare_row[:, 0:1],
                              ALU.mult, ALU.add).then_inc(dst_ready, 1)
            dve.tensor_scalar(spare_less_dst[0:TAIL, TILES:TILES + 1], dst_f[0:TAIL, TILES:TILES + 1], -1.0,
                              spare_row[0:TAIL, 0:1], ALU.mult, ALU.add).then_inc(dst_ready, 1)
            dve.wait_ge(dst_ready, 7)

            def step(r, u):
                t = tile_of(r, u)
                n = rows(t)
                dve.tensor_copy(tile_dst[0:n, u:u + 1], dst_f[0:n, bass.ds(t, 1)]).then_inc(dst_placed, 1)
                dve.wait_ge(dst_spread, t + 1)
                dve.tensor_scalar(same[0:n, u, 0:n], dst_ps[u][0:n, 0:n], tile_dst[0:n, u:u + 1], None,
                                  ALU.is_equal).then_inc(same_done, 1)
                dve.wait_ge(same_done, t + 1)
                dve.tensor_tensor_reduce(earlier[0:n, u, 0:n], same[0:n, u, 0:n], lower[0:n, 0:n], 1.0, 0.0,
                                         ALU.mult, ALU.add, n_earlier[0:n, u:u + 1]).then_inc(step_done, 1)
                dve.wait_ge(step_done, 2 * t + 1)
                dve.tensor_scalar(repeated[0:n, u:u + 1], n_earlier[0:n, u:u + 1], 0.5, None,
                                  ALU.is_ge).then_inc(step_done, 1)
                dve.wait_ge(step_done, 2 * t + 2)
                if not (isinstance(r, int) and r == 0):
                    dve.wait_ge(scattered, 16 * (t - UNROLL + 1))
                dve.tensor_scalar(row_idx[0:n, u, :], spare_less_dst[0:n, bass.ds(t, 1)], repeated[0:n, u:u + 1],
                                  tile_dst[0:n, u:u + 1], ALU.mult, ALU.add).then_inc(row_done, 1)
                dve.wait_ge(msg_done, t + 1)
                dve.tensor_copy(msg[0:n, u, :], msg_ps[u][0:n, :]).then_inc(msg_copied, 1)
                dve.wait_ge(sum_done, t + 1)
                dve.tensor_copy(sums[0:n, u, :], sum_ps[u][0:n, :]).then_inc(sum_copied, 1)

            tiles(dve, step)
            for c in range(CHUNKS + 1):
                s, n, g = c % LN_SLOTS, ln_rows(c), ln_cols(c)
                xc = xa[0:n, s, 0:g, :]
                dve.wait_ge(chunk_in[s], 16 * (c // LN_SLOTS + 1))
                if c >= LN_SLOTS:
                    dve.wait_ge(std_done, c - LN_SLOTS + 1)
                    dve.wait_ge(normed, c - LN_SLOTS + 1)
                dve.tensor_reduce(mean[0:n, s, 0:g], xc, AX_X, ALU.add).then_inc(ln_step, 1)
                dve.wait_ge(ln_step, 2 * c + 1)
                dve.tensor_scalar(mean[0:n, s, 0:g], mean[0:n, s, 0:g], 1.0 / D, None, ALU.mult).then_inc(ln_step, 1)
                dve.wait_ge(ln_step, 2 * c + 2)
                dve.tensor_tensor(xc, xc, mean[0:n, s, 0:g].unsqueeze(2).broadcast_to([n, g, D]),
                                  ALU.subtract).then_inc(centred, 1)
                dve.wait_ge(squared, c + 1)
                dve.tensor_reduce(var[0:n, s, 0:g], xsq[0:n, s, 0:g, :], AX_X, ALU.add).then_inc(var_done, 1)
                dve.wait_ge(std_done, c + 1)
                dve.reciprocal(rstd[0:n, s, 0:g], std[0:n, s, 0:g]).then_inc(rstd_done, 1)


_INS = ['x', 'src', 'dst', 'edge_attr_32', 'L0_gnn_W1', 'L0_gnn_b1', 'L0_gnn_W2', 'L0_gnn_b2']


def kernel(**inputs):
    import numpy as _np
    import concourse.bacc as _bacc
    from concourse import mybir as _mybir
    from concourse.bass_utils import run_bass_kernel_spmd as _run

    nc = _bacc.Bacc("TRN2", target_bir_lowering=False, num_devices=1)
    arrays, args = {}, []
    for name in _INS:
        a = _np.ascontiguousarray(inputs[name])
        arrays[f"in_{name}_dram"] = a
        args.append(nc.dram_tensor(f"in_{name}_dram", a.shape, _mybir.dt.from_np(a.dtype), kind="ExternalInput").ap())
    shape = _np.asarray(inputs['x']).shape
    args.append(nc.dram_tensor("out_0_dram", shape, _mybir.dt.float32, kind="ExternalOutput").ap())
    gnn_resnorm_kernel(nc, *args)
    r = _run(nc, [arrays], core_ids=[0])
    return r.results[0]["out_0_dram"]
```

```python
from contextlib import ExitStack

import concourse.bass as bass
from concourse import mybir

P = 128
F32 = mybir.dt.float32
I32 = mybir.dt.int32
BF16 = mybir.dt.bfloat16
F16 = mybir.dt.float16
ALU = mybir.AluOpType
ACT = mybir.ActivationFunctionType
AX_X = mybir.AxisListType.X
EPS = 1e-5
META = 2

J = 3
BP = 128
BLOCK = BP * J
SUPER = 3
BODY = 6
SMALL = 2
X_SLOTS = 3
AHEAD = 3
PEELED = 2
PARTS = 3

UNROLL = 5
SCATTER_LAG = 2
LN_SLOTS = 2


def general_path(nc, ctx, given):
    x, src, dst, edge_attr, out, acc, w1, w2, b1c, b2b, ident, eps, bank, general, general_done = (given[k] for k in (
        "x", "src", "dst", "edge_attr", "out", "acc", "w1", "w2", "b1c", "b2b", "ident", "eps", "bank", "general", "general_done"))
    N, D = x.shape
    E, DE = edge_attr.shape
    TILES = E // P
    TAIL = E - TILES * P
    TROUNDS = TILES // UNROLL
    assert TROUNDS * UNROLL == TILES and TROUNDS > 2 and TAIL > 0
    PER = N // P
    NREST = N - PER * P
    CHUNKS = 11
    G = PER // CHUNKS
    assert G * CHUNKS == PER and NREST > 0 and (N * D) % (3 * P) == 0

    def sb(name, shape, dt=F32):
        return ctx.enter_context(nc.sbuf_tensor("g_" + name, shape, dt))

    def sem(name):
        return ctx.enter_context(nc.semaphore("g_" + name))

    src_idx = sb("src_idx", [P, TILES + 1], I32)
    dst_idx = sb("dst_idx", [P, TILES + 1], I32)
    node_idx = sb("node_idx", [P, TILES + UNROLL, 2], I32)
    tile_idx = sb("tile_idx", [P, UNROLL, 2], I32)
    dst_f = sb("dst_f", [P, TILES + 1])
    tile_dst = sb("tile_dst", [P, UNROLL])
    spare_less_dst = sb("spare_less_dst", [P, TILES + 1])
    spare_row_i = sb("spare_row_i", [P, 1], I32)
    spare_row = sb("spare_row", [P, 1])
    lower = sb("lower", [P, P])
    cat = sb("cat", [P, UNROLL, P])
    cat_t = sb("cat_t", [P, UNROLL, P])
    hid_t = sb("hid_t", [P, UNROLL, P])
    msg = sb("msg", [P, UNROLL, D])
    same = sb("same", [P, UNROLL, P])
    earlier = sb("earlier", [P, UNROLL, P])
    n_earlier = sb("n_earlier", [P, UNROLL])
    repeated = sb("repeated", [P, UNROLL])
    row_idx = sb("row_idx", [P, UNROLL, 1], I32)
    sums = sb("sums", [P, UNROLL, D])
    cat_ps = [b[:, 0:P] for b in bank[0:UNROLL]]
    hid_ps = [b[:, P:2 * P] for b in bank[0:UNROLL]]
    dst_ps = [b[:, 2 * P:3 * P] for b in bank[0:UNROLL]]
    msg_ps = [b[:, 3 * P:3 * P + D] for b in bank[0:UNROLL]]
    sum_ps = [b[:, 3 * P + 64:3 * P + 64 + D] for b in bank[0:UNROLL]]
    xa = sb("xa", [P, LN_SLOTS, G, D])
    xsq = [given[k].rearrange("p t c -> p (t c)")[:, 0:G * D].rearrange("p (g d) -> p g d", d=D) for k in ("edge_pm", "table_pm")]
    mean = sb("mean", [P, LN_SLOTS, G])
    var = sb("var", [P, LN_SLOTS, G])
    std = sb("std", [P, LN_SLOTS, G])
    rstd = sb("rstd", [P, LN_SLOTS, G])

    idx_in = sem("idx_in")
    acc_start = sem("acc_start")
    consts = sem("consts")
    const_base = sem("const_base")
    dst_ready = sem("dst_ready")
    dst_placed = sem("dst_placed")
    may_gather = sem("may_gather")
    may_scatter = sem("may_scatter")
    idx_base = sem("idx_base")
    idx_paired = sem("idx_paired")
    idx_placed = sem("idx_placed")
    edge_in = [sem(f"edge_in{u}") for u in range(UNROLL)]
    xdst_in = [sem(f"xdst_in{u}") for u in range(UNROLL)]
    xsrc_in = [sem(f"xsrc_in{u}") for u in range(UNROLL)]
    cat_placed = sem("cat_placed")
    cat_copied = sem("cat_copied")
    hid_done = sem("hid_done")
    relu_done = sem("relu_done")
    msg_done = sem("msg_done")
    msg_copied = sem("msg_copied")
    dst_spread = sem("dst_spread")
    same_done = sem("same_done")
    step_done = sem("step_done")
    row_done = sem("row_done")
    sum_done = sem("sum_done")
    sum_copied = sem("sum_copied")
    scattered = sem("scattered")
    chunk_in = [sem(f"chunk_in{s}") for s in range(LN_SLOTS)]
    mean_done = sem("mean_done")
    centred = sem("centred")
    squared = sem("squared")
    var_done = sem("var_done")
    std_done = sem("std_done")
    rstd_done = sem("rstd_done")
    normed = sem("normed")
    ln_step = sem("ln_step")
    chunk_out = [sem(f"chunk_out{s}") for s in range(LN_SLOTS)]

    main = TILES * P
    src_v = src[0:main].rearrange("(p t) -> p t", p=P)
    dst_v = dst[0:main].rearrange("(p t) -> p t", p=P)
    edge_v = edge_attr[0:main, :].rearrange("(p t) d -> p t d", p=P)

    def rows(t):
        return TAIL if isinstance(t, int) and t == TILES else P

    def tiles(eng, step):
        for u in range(UNROLL):
            step(0, u)
        with eng.Fori(1, TROUNDS) as r:
            for u in range(UNROLL):
                step(r, u)
        step(TROUNDS, 0)

    def tile_of(r, u):
        return r * UNROLL + u

    def ln_rows(c):
        return P if c < CHUNKS else NREST

    def ln_cols(c):
        return G if c < CHUNKS else 1

    def ln_pair(c, table, tile):
        s = c % LN_SLOTS
        if c < CHUNKS:
            t = table[0:PER * P, :].rearrange("(p j) d -> p j d", p=P)[:, c * G:(c + 1) * G, :]
            return t, tile[:, s, :, :]
        return table[PER * P:N, :], tile[0:NREST, s, 0, :]

    def sync(sp):
        sp.dma_start(dst_idx[:, 0:TILES], dst_v).then_inc(idx_in, 16)
        sp.dma_start(src_idx[:, 0:TILES], src_v).then_inc(idx_in, 16)
        sp.dma_start(dst_idx[0:TAIL, TILES:TILES + 1], dst[main:E].rearrange("(p t) -> p t", t=1)).then_inc(idx_in, 16)
        sp.dma_start(src_idx[0:TAIL, TILES:TILES + 1], src[main:E].rearrange("(p t) -> p t", t=1)).then_inc(idx_in, 16)

        def load_edges(r, u):
            t = tile_of(r, u)
            n = rows(t)
            if not (isinstance(r, int) and r == 0):
                sp.wait_ge(cat_placed, t - UNROLL + 1)
            source = edge_attr[main:E, :] if n == TAIL else edge_v[:, bass.ds(t, 1), :].rearrange("p t d -> p (t d)")
            sp.dma_start(cat[0:n, u, 2 * D:P], source).then_inc(edge_in[u], 16)

        tiles(sp, load_edges)
        sp.wait_ge(scattered, 16 * (TILES + 1))
        for c in range(CHUNKS + 1):
            s = c % LN_SLOTS
            if c >= LN_SLOTS:
                sp.wait_ge(chunk_out[s], 16 * (c // LN_SLOTS))
            sp.dma_start(*ln_pair(c, acc, xa)[::-1]).then_inc(chunk_in[s], 16)

    def gpsimd(pool):
        pool.memset(lower[:, :], 1.0).then_inc(const_base, 1)
        pool.wait_ge(const_base, 1)
        pool.affine_select(out=lower[:, :], in_=lower[:, :], pattern=[[-1, P]], compare_op=ALU.is_gt,
                           fill=0.0, base=0, channel_multiplier=1).then_inc(consts, 1)
        pool.iota(spare_row_i[:, :], pattern=[[0, 1]], base=N, channel_multiplier=1).then_inc(consts, 1)

        def gather(r, u):
            t = tile_of(r, u)
            n = rows(t)
            if not (isinstance(r, int) and r == 0):
                pool.wait_ge(cat_placed, t - UNROLL + 1)
            pool.wait_ge(idx_placed, t + 1)
            pool.sem_inc(may_gather, 1)
            pool.indirect_dma_start(cat[0:n, u, 0:D], None, x[:, :],
                                    bass.IndirectOffsetOnAxis(ap=tile_idx[0:n, u, 0:1], axis=0)).then_inc(xdst_in[u], 16)
            pool.indirect_dma_start(cat[0:n, u, D:2 * D], None, x[:, :],
                                    bass.IndirectOffsetOnAxis(ap=tile_idx[0:n, u, 1:2], axis=0)).then_inc(xsrc_in[u], 16)

        def scatter(t, u):
            n = rows(t)
            pool.wait_ge(sum_copied, t + 1)
            pool.wait_ge(row_done, t + 1)
            if not (isinstance(t, int) and t == 0):
                pool.wait_ge(scattered, 16 * t)
            pool.sem_inc(may_scatter, 1)
            pool.indirect_dma_start(acc[:, :], bass.IndirectOffsetOnAxis(ap=row_idx[0:n, u, :], axis=0),
                                    sums[0:n, u, :], None, compute_op=ALU.add).then_inc(scattered, 16)

        for u in range(UNROLL):
            gather(0, u)
            if u == SCATTER_LAG:
                pool.wait_ge(acc_start, 32)
            if u >= SCATTER_LAG:
                scatter(u - SCATTER_LAG, u - SCATTER_LAG)
        with pool.Fori(1, TROUNDS) as r:
            for u in range(UNROLL):
                gather(r, u)
                scatter(tile_of(r, u) - SCATTER_LAG, (u - SCATTER_LAG) % UNROLL)
        gather(TROUNDS, 0)
        for t in range(TILES - SCATTER_LAG, TILES + 1):
            scatter(t, t % UNROLL)
        for c in range(CHUNKS + 1):
            s, n, g = c % LN_SLOTS, ln_rows(c), ln_cols(c)
            pool.wait_ge(rstd_done, c + 1)
            pool.tensor_tensor(xa[0:n, s, 0:g, :], xa[0:n, s, 0:g, :],
                               rstd[0:n, s, 0:g].unsqueeze(2).broadcast_to([n, g, D]), ALU.mult).then_inc(normed, 1)

    def tensor(pe):

        def step(r, u):
            t = tile_of(r, u)
            n = rows(t)
            first = isinstance(r, int) and r == 0
            if not first:
                pe.wait_ge(sum_copied, t - UNROLL + 1)
            pe.wait_ge(dst_placed, t + 1)
            pe.transpose(dst_ps[u][0:n, 0:n], tile_dst[0:n, u:u + 1].broadcast_to([n, n]),
                         ident[0:n, 0:n]).then_inc(dst_spread, 1)
            rr = 16 * (r + 1)
            pe.wait_ge(edge_in[u], rr)
            pe.wait_ge(xdst_in[u], rr)
            pe.wait_ge(xsrc_in[u], rr)
            pe.wait_ge(same_done, t + 1)
            pe.transpose(cat_ps[u][:, 0:n], cat[0:n, u, :], ident[0:n, 0:n]).then_inc(cat_placed, 1)
            pe.wait_ge(cat_copied, t + 1)
            pe.matmul(hid_ps[u][:, 0:n], w1[:, :], cat_t[:, u, 0:n], start=True, stop=True).then_inc(hid_done, 1)
            pe.wait_ge(relu_done, t + 1)
            pe.matmul(msg_ps[u][0:n, :], hid_t[:, u, 0:n], w2[:, :], start=True, stop=True).then_inc(msg_done, 1)
            pe.wait_ge(msg_copied, t + 1)
            pe.matmul(sum_ps[u][0:n, :], same[0:n, u, 0:n], msg[0:n, u, :], start=True, stop=True).then_inc(sum_done, 1)

        tiles(pe, step)

    def scalar(act):
        flat_x = x.rearrange("n d -> (n d)").rearrange("(k m) -> k m", k=3 * P)
        flat_a = acc[0:N, :].rearrange("n d -> (n d)").rearrange("(k m) -> k m", k=3 * P)
        act.dma_start(flat_a, flat_x).then_inc(acc_start, 16)
        act.dma_start(acc[N:N + P, :], x[0:P, :]).then_inc(acc_start, 16)
        act.wait_ge(idx_paired, 4)
        for t in range(UNROLL - 1):
            act.activation(tile_idx[:, t, :], node_idx[:, t, :], ACT.Copy).then_inc(idx_placed, 1)

        def step(r, u):
            t = tile_of(r, u)
            n = rows(t)
            act.wait_ge(cat_placed, t + 1)
            act.activation(cat_t[:, u, 0:n], cat_ps[u][:, 0:n], ACT.Copy).then_inc(cat_copied, 1)
            if not (isinstance(r, int) and r == TROUNDS):
                act.activation(tile_idx[:, (u - 1) % UNROLL, :],
                               node_idx[:, bass.ds(t + UNROLL - 1, 1), :].rearrange("p t k -> p (t k)"),
                               ACT.Copy).then_inc(idx_placed, 1)
            act.wait_ge(hid_done, t + 1)
            act.activation(hid_t[:, u, 0:n], hid_ps[u][:, 0:n], ACT.Relu, bias=b1c[:, 0:1]).then_inc(relu_done, 1)

        tiles(act, step)
        for c in range(CHUNKS + 2):
            if c <= CHUNKS:
                s, n, g = c % LN_SLOTS, ln_rows(c), ln_cols(c)
                act.wait_ge(centred, c + 1)
                if c >= LN_SLOTS:
                    act.wait_ge(var_done, c - LN_SLOTS + 1)
                act.activation(xsq[s][0:n, 0:g, :], xa[0:n, s, 0:g, :], ACT.Square).then_inc(squared, 1)
                act.wait_ge(var_done, c + 1)
                act.activation(std[0:n, s, 0:g], var[0:n, s, 0:g], ACT.Sqrt, bias=eps[0:n, 0:1],
                               scale=1.0 / D).then_inc(std_done, 1)
            if c >= 1:
                act.wait_ge(normed, c)
                act.dma_start(*ln_pair(c - 1, out, xa)).then_inc(chunk_out[(c - 1) % LN_SLOTS], 16)
        for s in range(LN_SLOTS):
            act.wait_ge(chunk_out[s], 16 * len(range(s, CHUNKS + 1, LN_SLOTS)))

    def vector(dve):
        dve.memset(node_idx[:, TILES:TILES + UNROLL, :], 0).then_inc(idx_base, 1)
        dve.wait_ge(idx_in, 64)
        dve.wait_ge(idx_base, 1)
        for k, idx in enumerate((dst_idx, src_idx)):
            dve.tensor_copy(node_idx[:, 0:TILES, k], idx[:, 0:TILES]).then_inc(idx_paired, 1)
            dve.tensor_copy(node_idx[0:TAIL, TILES, k:k + 1], idx[0:TAIL, TILES:TILES + 1]).then_inc(idx_paired, 1)
        dve.wait_ge(consts, 2)
        dve.tensor_copy(spare_row[:, :], spare_row_i[:, :]).then_inc(dst_ready, 1)
        dve.tensor_copy(dst_f[:, 0:TILES], dst_idx[:, 0:TILES]).then_inc(dst_ready, 1)
        dve.tensor_copy(dst_f[0:TAIL, TILES:TILES + 1], dst_idx[0:TAIL, TILES:TILES + 1]).then_inc(dst_ready, 1)
        dve.wait_ge(dst_ready, 3)
        dve.tensor_scalar(spare_less_dst[:, 0:TILES], dst_f[:, 0:TILES], -1.0, spare_row[:, 0:1],
                          ALU.mult, ALU.add).then_inc(dst_ready, 1)
        dve.tensor_scalar(spare_less_dst[0:TAIL, TILES:TILES + 1], dst_f[0:TAIL, TILES:TILES + 1], -1.0,
                          spare_row[0:TAIL, 0:1], ALU.mult, ALU.add).then_inc(dst_ready, 1)
        dve.wait_ge(dst_ready, 5)

        def step(r, u):
            t = tile_of(r, u)
            n = rows(t)
            dve.tensor_copy(tile_dst[0:n, u:u + 1], dst_f[0:n, bass.ds(t, 1)]).then_inc(dst_placed, 1)
            dve.wait_ge(dst_spread, t + 1)
            dve.tensor_scalar(same[0:n, u, 0:n], dst_ps[u][0:n, 0:n], tile_dst[0:n, u:u + 1], None,
                              ALU.is_equal).then_inc(same_done, 1)
            dve.wait_ge(same_done, t + 1)
            dve.tensor_tensor_reduce(earlier[0:n, u, 0:n], same[0:n, u, 0:n], lower[0:n, 0:n], 1.0, 0.0,
                                     ALU.mult, ALU.add, n_earlier[0:n, u:u + 1]).then_inc(step_done, 1)
            dve.wait_ge(step_done, 2 * t + 1)
            dve.tensor_scalar(repeated[0:n, u:u + 1], n_earlier[0:n, u:u + 1], 0.5, None,
                              ALU.is_ge).then_inc(step_done, 1)
            dve.wait_ge(step_done, 2 * t + 2)
            if not (isinstance(r, int) and r == 0):
                dve.wait_ge(scattered, 16 * (t - UNROLL + 1))
            dve.tensor_scalar(row_idx[0:n, u, :], spare_less_dst[0:n, bass.ds(t, 1)], repeated[0:n, u:u + 1],
                              tile_dst[0:n, u:u + 1], ALU.mult, ALU.add).then_inc(row_done, 1)
            dve.wait_ge(msg_done, t + 1)
            dve.tensor_tensor(msg[0:n, u, :], msg_ps[u][0:n, :], b2b[0:n, :], ALU.add).then_inc(msg_copied, 1)
            dve.wait_ge(sum_done, t + 1)
            dve.tensor_copy(sums[0:n, u, :], sum_ps[u][0:n, :]).then_inc(sum_copied, 1)

        tiles(dve, step)
        for c in range(CHUNKS + 1):
            s, n, g = c % LN_SLOTS, ln_rows(c), ln_cols(c)
            xc = xa[0:n, s, 0:g, :]
            dve.wait_ge(chunk_in[s], 16 * (c // LN_SLOTS + 1))
            if c >= LN_SLOTS:
                dve.wait_ge(std_done, c - LN_SLOTS + 1)
                dve.wait_ge(normed, c - LN_SLOTS + 1)
            dve.tensor_reduce(mean[0:n, s, 0:g], xc, AX_X, ALU.add).then_inc(ln_step, 1)
            dve.wait_ge(ln_step, 2 * c + 1)
            dve.tensor_scalar(mean[0:n, s, 0:g], mean[0:n, s, 0:g], 1.0 / D, None, ALU.mult).then_inc(ln_step, 1)
            dve.wait_ge(ln_step, 2 * c + 2)
            dve.tensor_tensor(xc, xc, mean[0:n, s, 0:g].unsqueeze(2).broadcast_to([n, g, D]),
                              ALU.subtract).then_inc(centred, 1)
            dve.wait_ge(squared, c + 1)
            dve.tensor_reduce(var[0:n, s, 0:g], xsq[s][0:n, 0:g, :], AX_X, ALU.add).then_inc(var_done, 1)
            dve.wait_ge(std_done, c + 1)
            dve.reciprocal(rstd[0:n, s, 0:g], std[0:n, s, 0:g]).then_inc(rstd_done, 1)

    return {"sync": sync, "gpsimd": gpsimd, "tensor": tensor, "scalar": scalar, "vector": vector}


def gnn_resnorm_kernel(nc, x, src, dst, edge_attr, W1, b1, W2, b2, out):
    N, D = x.shape
    E, DE = edge_attr.shape
    FIN, HID = W1.shape
    assert FIN == P and HID == P and 2 * D + DE == P

    FULL = N // BLOCK
    REST = N - FULL * BLOCK
    NB = FULL + 1
    RJ = 2
    RP = REST // RJ
    assert RP * RJ == REST and RP <= P and 0 < FULL % SUPER
    FULL_SUPERS = FULL // SUPER
    NS = FULL_SUPERS + 2
    ROUNDS = (FULL_SUPERS - AHEAD) // BODY
    LEFT = NS - ROUNDS * BODY
    SD = SUPER * J * D
    EC = -(-E // P)
    EP = E // EC
    EREST = E - EP * EC
    assert EP == P - 1 and 0 < EREST < EC
    EK = EP // 16 * 16
    ROWS = P * EC
    LAST = ROWS - P
    assert LAST + P >= E
    FAR = 1 << 20
    BG = 100
    NG = 3
    assert NG * BG >= NB + 1 and N < FAR

    edge_table = nc.dram_tensor("edge_table", (ROWS, DE + META), F32, kind="Internal").ap()
    acc = nc.dram_tensor("acc", (N + P, D), F32, kind="Internal").ap()

    with ExitStack() as ctx:
        def sb(name, shape, dt=F32):
            return ctx.enter_context(nc.sbuf_tensor(name, shape, dt))

        def sem(name):
            return ctx.enter_context(nc.semaphore(name))

        bank = [ctx.enter_context(nc.psum_tensor(f"bank{i}", [P, 512], F32)) for i in range(8)]

        ident = sb("ident", [P, P])
        ones = sb("ones", [P, P])
        w1 = sb("w1", [P, HID])
        b1c = sb("b1c", [HID, 1])
        w2 = sb("w2", [HID, D])
        b2b = sb("b2b", [P, D])
        eps = sb("eps", [P, 1])

        dst_pm = sb("dst_pm", [P, EC], I32)
        src_pm = sb("src_pm", [P, EC], I32)
        edge_pm = sb("edge_pm", [P, EC, DE])
        table_pm = sb("table_pm", [P, EC, DE + META])
        dst_rows = sb("dst_rows", [P, EC + 1])
        first_dst = sb("first_dst", [P, 1])
        next_dst_i = sb("next_dst_i", [P, 1], I32)
        next_dst = sb("next_dst", [P, 1])
        int_row = sb("int_row", [P, NG * BG], I32)
        bound_row = sb("bound_row", [P, NG * BG])
        int_col = sb("int_col", [P, 2], I32)
        bound_col = sb("bound_col", [P, NG])
        past_next = sb("past_next", [P, NG * BG])
        holder = sb("holder", [P, NG * BG])
        below = sb("below", [P, NG, EC])
        n_below = sb("n_below", [P, NG])
        first_col = sb("first_col", [P, NG])
        first_row = sb("first_row", [1, NG * BG])
        first_clamped = sb("first_clamped", [1, NG * BG])
        first_edge = sb("first_edge", [1, NG * BG], I32)
        counts = sb("counts", [1, NG * BG])
        most = sb("most", [1, 1])
        crowded = sb("crowded", [1, 1])
        falls = sb("falls", [P, EC])
        n_falls = sb("n_falls", [P, 2])
        unsorted = sb("unsorted", [P, 1])
        general_f = sb("general_f", [1, 1])
        general = sb("general", [1, 1], I32)

        ident_b = sb("ident_b", [P, P], BF16)
        node_of_i = sb("node_of_i", [P, BLOCK], I32)
        node_of = sb("node_of", [P, BLOCK], F16)
        short_node_of = sb("short_node_of", [P, REST], F16)
        block_start = sb("block_start", [P, NB])
        block_start_i = sb("block_start_i", [P, NB], I32)
        b2s = sb("b2s", [P, SUPER, D])
        cat = sb("cat", [P, BODY, SUPER, P + META])
        onehot = sb("onehot", [P, BODY, SUPER, BLOCK], BF16)
        onehot_t = sb("onehot_t", [P, SMALL, SUPER, J * P], BF16)
        cat_t = sb("cat_t", [P, SMALL, SUPER * P])
        hid_t = sb("hid_t", [P, SMALL, SUPER * P])
        msg = sb("msg", [P, SMALL, SUPER * D])
        msg_rest = sb("msg_rest", [P, SMALL, SUPER * D])
        msg_part = [sb(f"msg_part{i}", [P, SMALL, SUPER * D], BF16) for i in range(PARTS)]
        xs = sb("xs", [P, X_SLOTS, SD])
        x_rest = sb("x_rest", [P, SMALL, SD])
        x_part = [sb(f"x_part{i}", [P, BODY, SD], BF16) for i in range(PARTS)]
        ys = sb("ys", [P, BODY, SD])
        sq = sb("sq", [P, SMALL, SD])
        total = sb("total", [P, SMALL, SUPER * J])
        sq_total = sb("sq_total", [P, SMALL, SUPER * J])
        std = sb("std", [P, SMALL, SUPER * J])
        rstd = sb("rstd", [P, SMALL, SUPER * J])
        onehot_ps = [bank[i][:, :].bitcast(BF16) for i in range(2)]
        cat_ps, hid_ps, xdst_ps, msg_ps = bank[2], bank[3], bank[4], bank[5]
        sum_ps = bank[6:8]

        const_base = sem("const_base")
        consts = sem("consts")
        weights_in = sem("weights_in")
        pad_set = sem("pad_set")
        dst_in = sem("dst_in")
        src_in = sem("src_in")
        next_in = sem("next_in")
        attr_in = sem("attr_in")
        setup = sem("setup")
        table_part = sem("table_part")
        table_out = sem("table_out")
        holder_ready = sem("holder_ready")
        rows_ready = sem("rows_ready")
        first_ready = sem("first_ready")
        first_turned = sem("first_turned")
        fell_ready = sem("fell_ready")
        fell_summed = sem("fell_summed")
        first_done = sem("first_done")
        general_done = sem("general_done")
        row_in = [sem(f"row_in{s}") for s in range(BODY)]
        xsrc_in = [sem(f"xsrc_in{s}") for s in range(BODY)]
        x_in = [sem(f"x_in{s}") for s in range(X_SLOTS)]
        y_out = [sem(f"y_out{s}") for s in range(BODY)]
        may_gather = sem("may_gather")
        onehot_ready = sem("onehot_ready")
        onehot_turned = sem("onehot_turned")
        onehot_t_ready = sem("onehot_t_ready")
        xdst_done = sem("xdst_done")
        xdst_placed = sem("xdst_placed")
        cat_turned = sem("cat_turned")
        cat_t_ready = sem("cat_t_ready")
        hid_done = sem("hid_done")
        hid_t_ready = sem("hid_t_ready")
        msg_done = sem("msg_done")
        msg_ready = sem("msg_ready")
        msg_high = sem("msg_high")
        msg_less_high = sem("msg_less_high")
        msg_middle = sem("msg_middle")
        msg_low = sem("msg_low")
        x_high = sem("x_high")
        x_less_high = sem("x_less_high")
        x_middle = sem("x_middle")
        x_low = sem("x_low")
        sum_done = sem("sum_done")
        totalled = sem("totalled")
        centred = sem("centred")
        squared = sem("squared")
        sq_totalled = sem("sq_totalled")
        std_ready = sem("std_ready")
        rstd_ready = sem("rstd_ready")
        normed = sem("normed")

        def at(r, u, k):
            q, v = divmod(u + k, BODY)
            return (r + q) * BODY + v, r + q, v

        def exists(g):
            return not isinstance(g, int) or 0 <= g < NS

        def after(g, k):
            return not isinstance(g, int) or g >= k

        def shape_of(g):
            if isinstance(g, int) and g == NS - 1:
                return RP, 1, RJ
            return BP, FULL % SUPER if isinstance(g, int) and g == NS - 2 else SUPER, J

        def first_block(g):
            return FULL if isinstance(g, int) and g == NS - 1 else g * SUPER

        def x_uses(r, v):
            return r * (BODY // X_SLOTS) + v // X_SLOTS + 1

        def walk(eng, step, before, extra):
            for u in range(-before, PEELED * BODY):
                step(u // BODY, u % BODY)
            with eng.Fori(PEELED, ROUNDS) as r:
                for u in range(BODY):
                    step(r, u)
            for k in range(LEFT + extra):
                step(ROUNDS + k // BODY, k % BODY)

        def dram_rows(table, g):
            n, blocks, jj = shape_of(g)
            if jj == RJ:
                return table[FULL * BLOCK:N, :].rearrange("(p j) d -> p (j d)", j=RJ)
            return table[0:FULL * BLOCK, :].rearrange("(b p j) d -> p b (j d)", p=BP, j=J)[:, bass.ds(g * SUPER, blocks), :]

        def sbuf_rows(tile, g, s):
            n, blocks, jj = shape_of(g)
            flat = tile[0:n, s, 0:blocks * jj * D]
            return flat if jj == RJ else flat.rearrange("p (b m) -> p b m", b=blocks)

        def flat_of(tile, g, s):
            n, blocks, jj = shape_of(g)
            return tile[0:n, s, 0:blocks * jj * D]

        def by_node(tile, g, s):
            return flat_of(tile, g, s).rearrange("p (m d) -> p m d", d=D)

        general_engine = general_path(nc, ctx, dict(
            x=x, src=src, dst=dst, edge_attr=edge_attr, out=out, acc=acc, w1=w1, w2=w2, b1c=b1c, b2b=b2b,
            ident=ident, eps=eps, bank=bank, edge_pm=edge_pm, table_pm=table_pm,
            general=general, general_done=general_done))
        block = ctx.enter_context(nc.Block())

        @block.sync
        def _(sp):
            sp.wait_ge(pad_set, 4)
            for table, idx, done in ((dst, dst_pm, dst_in), (src, src_pm, src_in)):
                full = table[0:EP * EC].rearrange("(p t) -> p t", p=EP)
                sp.dma_start(idx[0:EK, :], full[0:EK, :]).then_inc(done, 16)
                sp.dma_start(idx[EK:EP, :], full[EK:EP, :]).then_inc(done, 16)
                sp.dma_start(idx[EP:P, 0:EREST], table[EP * EC:E].rearrange("(a t) -> a t", a=1)).then_inc(done, 16)
            sp.dma_start(next_dst_i[0:EP, :], dst[EC:E].rearrange("(p t) -> p t", t=1)[0:(EP - 1) * EC + 1:EC, :],
                         allow_slow_non_contiguous=True).then_inc(next_in, 16)
            sp.dma_start(w1[:, :], W1).then_inc(weights_in, 16)
            sp.dma_start(w2[:, :], W2).then_inc(weights_in, 16)
            sp.dma_start(b1c[:, :], b1.rearrange("(p t) -> p t", t=1)).then_inc(weights_in, 16)
            sp.dma_start(b2b[:, :], b2.rearrange("(a d) -> a d", a=1).broadcast_to([P, D])).then_inc(weights_in, 16)
            sp.wait_ge(table_part, 4)
            sp.dma_start(edge_table.rearrange("(p t) c -> p (t c)", p=P),
                         table_pm[:, :, :].rearrange("p t c -> p (t c)")).then_inc(table_out, 16)
            sp.wait_ge(first_done, 1)
            sp.wait_ge(table_out, 16)

            def step(r, u):
                g, gr, gv = at(r, u, AHEAD)
                if exists(g):
                    n, blocks, jj = shape_of(g)
                    if after(g, X_SLOTS):
                        sp.wait_ge(x_less_high, g - X_SLOTS + 1)
                    sp.dma_start(sbuf_rows(xs, g, gv % X_SLOTS), dram_rows(x, g)).then_inc(x_in[gv % X_SLOTS], 16)
                    if after(g, BODY):
                        sp.wait_ge(cat_turned, g - BODY + 1)
                    for k in range(SUPER):
                        b = first_block(g) + min(k, blocks - 1)
                        first = sp.value_load(first_edge[0:1, bass.ds(b, 1)], min_val=0, max_val=LAST)
                        sp.dma_start(cat[:, gv, k, 2 * D:P + META], edge_table[bass.ds(first, P), :]).then_inc(row_in[gv], 16)
                g, gr, gv = at(r, u, -7)
                if exists(g):
                    sp.wait_ge(normed, g + 1)
                    sp.dma_start(dram_rows(out, g), sbuf_rows(ys, g, gv)).then_inc(y_out[gv], 16)

            walk(sp, step, AHEAD, 7)
            for s in range(BODY):
                sp.wait_ge(y_out[s], 16 * len(range(s, NS, BODY)))
            sp.wait_ge(general_done, 1)
            needed = sp.value_load(general[0:1, 0:1], min_val=0, max_val=1)
            with sp.If(needed > 0):
                general_engine["sync"](sp)

        @block.gpsimd
        def _(pool):
            pool.memset(ident[:, :], 0.0).then_inc(const_base, 1)
            pool.iota(int_row[:, :], pattern=[[BLOCK, NG * BG]], base=0, channel_multiplier=0).then_inc(consts, 1)
            pool.iota(int_col[:, 0:1], pattern=[[0, 1]], base=0, channel_multiplier=BLOCK).then_inc(consts, 1)
            pool.iota(int_col[:, 1:2], pattern=[[0, 1]], base=0, channel_multiplier=EC).then_inc(consts, 1)
            pool.iota(node_of_i[:, :], pattern=[[1, J], [J, BP]], base=0, channel_multiplier=0).then_inc(consts, 1)
            pool.wait_ge(const_base, 1)
            pool.affine_select(out=ident[:, :], in_=ident[:, :], pattern=[[-1, P]], compare_op=ALU.not_equal,
                               fill=1.0, base=0, channel_multiplier=1).then_inc(consts, 1)
            pool.wait_ge(setup, 1)
            pool.iota(node_of_i[:, 0:REST], pattern=[[1, RJ], [RJ, RP]], base=0, channel_multiplier=0).then_inc(consts, 1)
            pool.iota(block_start_i[:, :], pattern=[[BLOCK, NB]], base=0, channel_multiplier=0).then_inc(consts, 1)
            pool.wait_ge(attr_in, 48)
            pool.tensor_copy(table_pm[:, 0:EC // 2, 0:DE], edge_pm[:, 0:EC // 2, :]).then_inc(table_part, 1)

            def step(r, u):
                g, gr, gv = at(r, u, AHEAD - 1)
                if exists(g):
                    pool.wait_ge(row_in[gv], 16 * SUPER * (gr + 1))
                    pool.sem_inc(may_gather, 1)
                    for k in range(SUPER):
                        pool.indirect_dma_start(cat[:, gv, k, D:2 * D], None, x[:, :], bass.IndirectOffsetOnAxis(
                            ap=cat[:, gv, k, P + 1:P + 2].bitcast(I32), axis=0)).then_inc(xsrc_in[gv], 16)
                g, gr, gv = at(r, u, -6)
                if exists(g):
                    n, blocks, jj = shape_of(g)
                    y = by_node(ys, g, gv)
                    pool.wait_ge(rstd_ready, g + 1)
                    pool.tensor_tensor(y, y, rstd[0:n, gv % SMALL, 0:blocks * jj].unsqueeze(2).broadcast_to([n, blocks * jj, D]),
                                       ALU.mult).then_inc(normed, 1)

            walk(pool, step, AHEAD, 6)
            pool.wait_ge(general_done, 1)
            needed = pool.value_load(general[0:1, 0:1], min_val=0, max_val=1)
            with pool.If(needed > 0):
                general_engine["gpsimd"](pool)

        @block.tensor
        def _(pe):
            pe.wait_ge(consts, 5)
            pe.wait_ge(holder_ready, 1)
            for i in range(NG):
                pe.matmul(bank[i][0:BG, 0:EC + 1], holder[:, i * BG:(i + 1) * BG], dst_rows[:, :],
                          start=True, stop=True).then_inc(rows_ready, 1)
            pe.wait_ge(fell_ready, 1)
            pe.matmul(bank[3][0:1, 0:1], unsorted[:, :], ones[:, 0:1], start=True, stop=True).then_inc(fell_summed, 1)
            pe.wait_ge(first_ready, NG)
            for i in range(NG):
                pe.transpose(bank[4][0:1, i * BG:(i + 1) * BG], first_col[0:BG, i:i + 1],
                             ident[0:BG, 0:BG]).then_inc(first_turned, 1)
            pe.wait_ge(weights_in, 64)
            pe.wait_ge(general_done, 1)
            pe.wait_ge(setup, 2)

            def turn_cat(g, r, v):
                n, blocks, jj = shape_of(g)
                pe.wait_ge(xdst_placed, g + 1)
                pe.wait_ge(xsrc_in[v], 16 * SUPER * (r + 1))
                for k in range(blocks):
                    last = pe.transpose(cat_ps[:, k * P:(k + 1) * P], cat[:, v, k, 0:P], ident[:, :])
                last.then_inc(cat_turned, 1)

            def turn_onehot(g, r, v, ks):
                n, blocks, jj = shape_of(g)
                pe.wait_ge(onehot_ready, g + 1)
                for k in ks:
                    if k >= blocks:
                        continue
                    if k == 2:
                        pe.wait_ge(onehot_t_ready, first_block(g) + 1)
                    for j in range(jj):
                        last = pe.transpose(onehot_ps[k % 2][0:n, j * P:(j + 1) * P], onehot[:, v, k, j * n:(j + 1) * n],
                                            ident_b[:, :])
                    last.then_inc(onehot_turned, 1)

            def sums(g, r, v):
                n, blocks, jj = shape_of(g)
                ps, part_slot = sum_ps[v % SMALL], v % SMALL
                pe.wait_ge(msg_low, g + 1)
                if after(g, SMALL):
                    pe.wait_ge(centred, g - SMALL + 1)
                for i in range(PARTS):
                    pe.matmul(ps[0:n, 0:blocks * jj * D], ident_b[0:n, 0:n], flat_of(x_part[i], g, v),
                              start=(i == 0), stop=False)
                for k in range(blocks):
                    for j in range(jj):
                        for i in range(PARTS):
                            last = pe.matmul(ps[0:n, (k * jj + j) * D:(k * jj + j + 1) * D], onehot[:, v, k, j * n:(j + 1) * n],
                                             msg_part[i][:, part_slot, k * D:(k + 1) * D], start=False,
                                             stop=(k == blocks - 1 and j == jj - 1 and i == PARTS - 1))
                last.then_inc(sum_done, 1)

            def hidden(g, r, v):
                n, blocks, jj = shape_of(g)
                pe.wait_ge(cat_t_ready, g + 1)
                pe.matmul(hid_ps[:, 0:blocks * P], w1[:, :], cat_t[:, v % SMALL, 0:blocks * P],
                          start=True, stop=True).then_inc(hid_done, 1)

            def fetch_xdst(g, r, v):
                n, blocks, jj = shape_of(g)
                pe.wait_ge(x_low, g + 1)
                for k in range(blocks):
                    pe.wait_ge(onehot_t_ready, first_block(g) + k + 1)
                    for j in range(jj):
                        for i in range(PARTS):
                            last = pe.matmul(xdst_ps[:, k * D:(k + 1) * D], onehot_t[0:n, v % SMALL, k, j * P:(j + 1) * P],
                                             flat_of(x_part[i], g, v)[:, (k * jj + j) * D:(k * jj + j + 1) * D],
                                             start=(j == 0 and i == 0), stop=(j == jj - 1 and i == PARTS - 1))
                last.then_inc(xdst_done, 1)

            def messages(g, r, v):
                n, blocks, jj = shape_of(g)
                pe.wait_ge(hid_t_ready, g + 1)
                if after(g, 1):
                    pe.wait_ge(msg_ready, g)
                for k in range(blocks):
                    last = pe.matmul(msg_ps[:, k * D:(k + 1) * D], hid_t[:, v % SMALL, k * P:(k + 1) * P], w2[:, :],
                                     start=True, stop=True)
                last.then_inc(msg_done, 1)

            def step(r, u):
                for k, stage, more in ((1, turn_cat, ()), (0, turn_onehot, ((0, 1),)), (3, sums, ()), (0, turn_onehot, ((2,),)),
                                       (1, hidden, ()), (0, fetch_xdst, ()), (1, messages, ())):
                    g, gr, gv = at(r, u, -k)
                    if exists(g):
                        stage(g, gr, gv, *more)

            walk(pe, step, 0, 3)
            pe.wait_ge(general_done, 1)
            needed = pe.value_load(general[0:1, 0:1], min_val=0, max_val=1)
            with pe.If(needed > 0):
                general_engine["tensor"](pe)

        @block.scalar
        def _(act):
            attr_v = edge_attr[0:EP * EC, :].rearrange("(p t) d -> p t d", p=EP)
            act.wait_ge(pad_set, 4)
            act.dma_start(edge_pm[0:EK, :, :], attr_v[0:EK, :, :]).then_inc(attr_in, 16)
            act.dma_start(edge_pm[EK:EP, :, :], attr_v[EK:EP, :, :]).then_inc(attr_in, 16)
            act.dma_start(edge_pm[EP:P, 0:EREST, :], edge_attr[EP * EC:E, :].rearrange("(a t) d -> a t d", a=1)).then_inc(attr_in, 16)
            act.wait_ge(src_in, 48)
            act.activation(table_pm[:, :, DE + 1].bitcast(I32), src_pm[:, :], ACT.Copy).then_inc(table_part, 1)
            act.wait_ge(attr_in, 48)
            act.activation(table_pm[:, EC // 2:EC, 0:DE], edge_pm[:, EC // 2:EC, :], ACT.Copy).then_inc(table_part, 1)
            act.wait_ge(weights_in, 64)

            def copy_cat(g, r, v):
                n, blocks, jj = shape_of(g)
                act.wait_ge(cat_turned, g + 1)
                act.activation(cat_t[:, v % SMALL, 0:blocks * P], cat_ps[:, 0:blocks * P], ACT.Copy).then_inc(cat_t_ready, 1)

            def split_msg_high(g, r, v):
                n, blocks, jj = shape_of(g)
                act.wait_ge(msg_ready, g + 1)
                if after(g, SMALL):
                    act.wait_ge(sum_done, g - SMALL + 1)
                act.activation(msg_part[0][:, v % SMALL, 0:blocks * D], msg[:, v % SMALL, 0:blocks * D],
                               ACT.Copy).then_inc(msg_high, 1)

            def split_msg_middle(g, r, v):
                n, blocks, jj = shape_of(g)
                act.wait_ge(msg_less_high, g + 1)
                act.activation(msg_part[1][:, v % SMALL, 0:blocks * D], msg_rest[:, v % SMALL, 0:blocks * D],
                               ACT.Copy).then_inc(msg_middle, 1)

            def copy_onehot(g, r, v, ks):
                n, blocks, jj = shape_of(g)
                for k in ks:
                    if k < blocks:
                        act.wait_ge(onehot_turned, first_block(g) + k + 1)
                        act.activation(onehot_t[0:n, v % SMALL, k, 0:jj * P], onehot_ps[k % 2][0:n, 0:jj * P],
                                       ACT.Copy).then_inc(onehot_t_ready, 1)

            def split_x_high(g, r, v):
                act.wait_ge(x_in[v % X_SLOTS], 16 * x_uses(r, v))
                if after(g, BODY):
                    act.wait_ge(sum_done, g - BODY + 1)
                act.activation(flat_of(x_part[0], g, v), flat_of(xs, g, v % X_SLOTS), ACT.Copy).then_inc(x_high, 1)

            def split_x_middle(g, r, v):
                act.wait_ge(x_less_high, g + 1)
                act.activation(flat_of(x_part[1], g, v), flat_of(x_rest, g, v % SMALL), ACT.Copy).then_inc(x_middle, 1)

            def relu(g, r, v):
                n, blocks, jj = shape_of(g)
                act.wait_ge(hid_done, g + 1)
                act.activation(hid_t[:, v % SMALL, 0:blocks * P], hid_ps[:, 0:blocks * P], ACT.Relu,
                               bias=b1c[:, 0:1]).then_inc(hid_t_ready, 1)

            def place_xdst(g, r, v):
                n, blocks, jj = shape_of(g)
                act.wait_ge(xdst_done, g + 1)
                act.activation(cat[:, v, 0:blocks, 0:D], xdst_ps[:, 0:blocks * D].rearrange("p (b d) -> p b d", d=D),
                               ACT.Copy).then_inc(xdst_placed, 1)

            def square(g, r, v):
                act.wait_ge(centred, g + 1)
                act.activation(flat_of(sq, g, v % SMALL), flat_of(ys, g, v), ACT.Square).then_inc(squared, 1)

            def root(g, r, v):
                n, blocks, jj = shape_of(g)
                act.wait_ge(sq_totalled, g + 1)
                act.activation(std[0:n, v % SMALL, 0:blocks * jj], sq_total[0:n, v % SMALL, 0:blocks * jj], ACT.Sqrt,
                               bias=eps[0:n, 0:1], scale=1.0 / D).then_inc(std_ready, 1)

            def step(r, u):
                for k, stage, more in ((1, copy_cat, ()), (2, split_msg_high, ()), (0, copy_onehot, ((0, 1),)),
                                       (2, split_msg_middle, ()), (-1, split_x_high, ()), (0, copy_onehot, ((2,),)),
                                       (1, relu, ()), (-1, split_x_middle, ()), (4, square, ()), (0, place_xdst, ()),
                                       (6, root, ())):
                    g, gr, gv = at(r, u, -k)
                    if exists(g):
                        stage(g, gr, gv, *more)

            walk(act, step, 1, 6)
            act.wait_ge(general_done, 1)
            needed = act.value_load(general[0:1, 0:1], min_val=0, max_val=1)
            with act.If(needed > 0):
                general_engine["scalar"](act)

        @block.vector
        def _(dve):
            n_setup = [0]

            def note(ins):
                n_setup[0] += 1
                ins.then_inc(setup, 1)
                dve.wait_ge(setup, n_setup[0])

            dve.memset(dst_pm[:, :], FAR).then_inc(pad_set, 1)
            dve.memset(src_pm[:, :], 0).then_inc(pad_set, 1)
            dve.memset(next_dst_i[:, :], FAR).then_inc(pad_set, 1)
            dve.memset(edge_pm[:, EREST:EC, :], 0.0).then_inc(pad_set, 1)
            dve.wait_ge(consts, 4)
            note(dve.tensor_copy(node_of[:, :], node_of_i[:, :]))
            dve.wait_ge(consts, 5)
            note(dve.tensor_copy(ident_b[:, :], ident[:, :]))
            note(dve.memset(ones[:, :], 1.0))
            note(dve.memset(eps[:, :], EPS))
            note(dve.tensor_copy(bound_row[:, :], int_row[:, :]))
            note(dve.tensor_copy(dst_rows[:, EC:EC + 1], int_col[:, 1:2]))
            for i in range(NG):
                note(dve.tensor_scalar(bound_col[:, i:i + 1], int_col[:, 0:1], float(i * BG * BLOCK), None, ALU.add))
            dve.wait_ge(dst_in, 48)
            note(dve.tensor_copy(dst_rows[:, 0:EC], dst_pm[:, :]))
            dve.wait_ge(next_in, 16)
            note(dve.tensor_copy(next_dst[:, :], next_dst_i[:, :]))
            note(dve.tensor_copy(first_dst[:, :], dst_rows[:, 0:1]))
            note(dve.memset(first_dst[0:1, :], -1.0))
            note(dve.tensor_scalar(past_next[:, :], bound_row[:, :], next_dst[:, 0:1], None, ALU.is_gt))
            dve.scalar_tensor_tensor(out=holder[:, :], in0=bound_row[:, :], scalar=first_dst[:, 0:1], in1=past_next[:, :],
                                     op0=ALU.is_gt, op1=ALU.subtract).then_inc(holder_ready, 1)
            dve.tensor_copy(table_pm[:, :, DE], dst_rows[:, 0:EC]).then_inc(table_part, 1)
            note(dve.tensor_tensor(falls[:, 0:EC - 1], dst_rows[:, 0:EC - 1], dst_rows[:, 1:EC], ALU.is_gt))
            note(dve.tensor_tensor(falls[:, EC - 1:EC], dst_rows[:, EC - 1:EC], next_dst[:, :], ALU.is_gt))
            dve.tensor_reduce(unsorted[:, :], falls[:, :], AX_X, ALU.add).then_inc(fell_ready, 1)
            for i in range(NG):
                dve.wait_ge(rows_ready, i + 1)
                note(dve.tensor_scalar(below[0:BG, i, :], bank[i][0:BG, 0:EC], bound_col[0:BG, i:i + 1], None, ALU.is_lt))
                note(dve.tensor_reduce(n_below[0:BG, i:i + 1], below[0:BG, i, :], AX_X, ALU.add))
                dve.tensor_tensor(first_col[0:BG, i:i + 1], bank[i][0:BG, EC:EC + 1], n_below[0:BG, i:i + 1],
                                  ALU.add).then_inc(first_ready, 1)
            dve.wait_ge(first_turned, NG)
            note(dve.tensor_copy(first_row[:, :], bank[4][0:1, 0:NG * BG]))
            note(dve.tensor_scalar(first_clamped[:, :], first_row[:, :], 0.0, float(LAST), ALU.max, ALU.min))
            dve.tensor_copy(first_edge[:, :], first_clamped[:, :]).then_inc(first_done, 1)
            note(dve.tensor_tensor(counts[:, 0:NB], first_row[:, 1:NB + 1], first_row[:, 0:NB], ALU.subtract))
            note(dve.tensor_reduce(most[:, :], counts[:, 0:NB], AX_X, ALU.max))
            note(dve.tensor_scalar(crowded[:, :], most[:, :], P + 0.5, None, ALU.is_gt))
            dve.wait_ge(fell_summed, 1)
            note(dve.tensor_tensor(general_f[:, :], bank[3][0:1, 0:1], crowded[:, :], ALU.add))
            dve.tensor_scalar(general[:, :], general_f[:, :], 0.5, None, ALU.is_gt).then_inc(general_done, 1)
            dve.wait_ge(consts, 7)
            note(dve.tensor_copy(short_node_of[:, :], node_of_i[:, 0:REST]))
            note(dve.tensor_copy(block_start[:, :], block_start_i[:, :]))
            dve.wait_ge(weights_in, 64)
            for k in range(SUPER):
                note(dve.tensor_copy(b2s[:, k, :], b2b[:, :]))

            def copy_msg(g, r, v):
                n, blocks, jj = shape_of(g)
                dve.wait_ge(msg_done, g + 1)
                dve.tensor_tensor(msg[:, v % SMALL, 0:blocks * D], msg_ps[:, 0:blocks * D],
                                  b2s[:, 0:blocks, :].rearrange("p b d -> p (b d)"), ALU.add).then_inc(msg_ready, 1)

            def centre(g, r, v):
                n, blocks, jj = shape_of(g)
                t, m = v % SMALL, blocks * jj
                z = sum_ps[t][0:n, 0:m * D].rearrange("p (m d) -> p m d", d=D)
                dve.wait_ge(sum_done, g + 1)
                dve.tensor_reduce(total[0:n, t, 0:m], z, AX_X, ALU.add).then_inc(totalled, 1)
                dve.wait_ge(totalled, g + 1)
                if after(g, BODY):
                    dve.wait_ge(y_out[v], 16 * r)
                dve.scalar_tensor_tensor(out=by_node(ys, g, v), in0=total[0:n, t, 0:m].unsqueeze(2).broadcast_to([n, m, D]),
                                         scalar=-1.0 / D, in1=z, op0=ALU.mult, op1=ALU.add).then_inc(centred, 1)

            def split_msg_rest(g, r, v):
                n, blocks, jj = shape_of(g)
                t, w = v % SMALL, blocks * D
                dve.wait_ge(msg_high, g + 1)
                dve.tensor_tensor(msg_rest[:, t, 0:w], msg[:, t, 0:w], msg_part[0][:, t, 0:w],
                                  ALU.subtract).then_inc(msg_less_high, 1)

            def split_msg_low(g, r, v):
                n, blocks, jj = shape_of(g)
                t, w = v % SMALL, blocks * D
                dve.wait_ge(msg_middle, g + 1)
                dve.tensor_tensor(msg_part[2][:, t, 0:w], msg_rest[:, t, 0:w], msg_part[1][:, t, 0:w],
                                  ALU.subtract).then_inc(msg_low, 1)

            def make_onehot(g, r, v):
                n, blocks, jj = shape_of(g)
                nodes = node_of if jj == J else short_node_of
                dve.wait_ge(row_in[v], 16 * SUPER * (r + 1))
                if after(g, BODY):
                    dve.wait_ge(sum_done, g - BODY + 1)
                for k in range(blocks):
                    last = dve.tensor_scalar(onehot[:, v, k, 0:n * jj], nodes[:, 0:n * jj],
                                             block_start[:, bass.ds(first_block(g) + k, 1)], cat[:, v, k, P:P + 1],
                                             ALU.add, ALU.is_equal)
                last.then_inc(onehot_ready, 1)

            def split_x_rest(g, r, v):
                dve.wait_ge(x_high, g + 1)
                dve.tensor_tensor(flat_of(x_rest, g, v % SMALL), flat_of(xs, g, v % X_SLOTS), flat_of(x_part[0], g, v),
                                  ALU.subtract).then_inc(x_less_high, 1)

            def split_x_low(g, r, v):
                dve.wait_ge(x_middle, g + 1)
                dve.tensor_tensor(flat_of(x_part[2], g, v), flat_of(x_rest, g, v % SMALL), flat_of(x_part[1], g, v),
                                  ALU.subtract).then_inc(x_low, 1)

            def total_squares(g, r, v):
                n, blocks, jj = shape_of(g)
                t = v % SMALL
                dve.wait_ge(squared, g + 1)
                dve.tensor_reduce(sq_total[0:n, t, 0:blocks * jj], by_node(sq, g, t), AX_X, ALU.add).then_inc(sq_totalled, 1)

            def invert(g, r, v):
                n, blocks, jj = shape_of(g)
                t, m = v % SMALL, blocks * jj
                dve.wait_ge(std_ready, g + 1)
                if after(g, SMALL):
                    dve.wait_ge(normed, g - SMALL + 1)
                dve.reciprocal(rstd[0:n, t, 0:m], std[0:n, t, 0:m]).then_inc(rstd_ready, 1)

            def step(r, u):
                for k, stage in ((2, copy_msg), (4, centre), (2, split_msg_rest), (-1, make_onehot), (2, split_msg_low),
                                 (-1, split_x_rest), (5, total_squares), (-1, split_x_low), (6, invert)):
                    g, gr, gv = at(r, u, -k)
                    if exists(g):
                        stage(g, gr, gv)

            walk(dve, step, 1, 6)
            dve.wait_ge(general_done, 1)
            needed = dve.value_load(general[0:1, 0:1], min_val=0, max_val=1)
            with dve.If(needed > 0):
                general_engine["vector"](dve)


_INS = ['x', 'src', 'dst', 'edge_attr_32', 'L0_gnn_W1', 'L0_gnn_b1', 'L0_gnn_W2', 'L0_gnn_b2']


def kernel(**inputs):
    import numpy as _np
    import concourse.bacc as _bacc
    from concourse import mybir as _mybir
    from concourse.bass_utils import run_bass_kernel_spmd as _run

    nc = _bacc.Bacc("TRN2", target_bir_lowering=False, num_devices=1)
    arrays, args = {}, []
    for name in _INS:
        a = _np.ascontiguousarray(inputs[name])
        arrays[f"in_{name}_dram"] = a
        args.append(nc.dram_tensor(f"in_{name}_dram", a.shape, _mybir.dt.from_np(a.dtype), kind="ExternalInput").ap())
    shape = _np.asarray(inputs['x']).shape
    args.append(nc.dram_tensor("out_0_dram", shape, _mybir.dt.float32, kind="ExternalOutput").ap())
    gnn_resnorm_kernel(nc, *args)
    r = _run(nc, [arrays], core_ids=[0])
    return r.results[0]["out_0_dram"]
```

```python
from contextlib import ExitStack

import concourse.bass as bass
from concourse import mybir

P = 128
F32 = mybir.dt.float32
I32 = mybir.dt.int32
BF16 = mybir.dt.bfloat16
F16 = mybir.dt.float16
ALU = mybir.AluOpType
ACT = mybir.ActivationFunctionType
AX_X = mybir.AxisListType.X
EPS = 1e-5
META = 2

J = 3
BP = 128
BLOCK = BP * J
SUPER = 3
BODY = 8
SMALL = 2
AHEAD = 3
X_AHEAD = 2
PEELED = 2
PARTS = 3
assert PARTS == SUPER

UNROLL = 5
SCATTER_LAG = 2
LN_SLOTS = 2


def general_path(nc, ctx, given):
    x, src, dst, edge_attr, out, acc, w1, w2, b1c, b2b, ident, eps, bank, general, general_done = (given[k] for k in (
        "x", "src", "dst", "edge_attr", "out", "acc", "w1", "w2", "b1c", "b2b", "ident", "eps", "bank", "general", "general_done"))
    N, D = x.shape
    E, DE = edge_attr.shape
    TILES = E // P
    TAIL = E - TILES * P
    TROUNDS = TILES // UNROLL
    assert TROUNDS * UNROLL == TILES and TROUNDS > 2 and TAIL > 0
    PER = N // P
    NREST = N - PER * P
    CHUNKS = 11
    G = PER // CHUNKS
    assert G * CHUNKS == PER and NREST > 0 and (N * D) % (3 * P) == 0

    def sb(name, shape, dt=F32):
        return ctx.enter_context(nc.sbuf_tensor("g_" + name, shape, dt))

    def sem(name):
        return ctx.enter_context(nc.semaphore("g_" + name))

    src_idx = sb("src_idx", [P, TILES + 1], I32)
    dst_idx = sb("dst_idx", [P, TILES + 1], I32)
    node_idx = sb("node_idx", [P, TILES + UNROLL, 2], I32)
    tile_idx = sb("tile_idx", [P, UNROLL, 2], I32)
    dst_f = sb("dst_f", [P, TILES + 1])
    tile_dst = sb("tile_dst", [P, UNROLL])
    spare_less_dst = sb("spare_less_dst", [P, TILES + 1])
    spare_row_i = sb("spare_row_i", [P, 1], I32)
    spare_row = sb("spare_row", [P, 1])
    lower = sb("lower", [P, P])
    cat = sb("cat", [P, UNROLL, P])
    cat_t = sb("cat_t", [P, UNROLL, P])
    hid_t = sb("hid_t", [P, UNROLL, P])
    msg = sb("msg", [P, UNROLL, D])
    same = sb("same", [P, UNROLL, P])
    earlier = sb("earlier", [P, UNROLL, P])
    n_earlier = sb("n_earlier", [P, UNROLL])
    repeated = sb("repeated", [P, UNROLL])
    row_idx = sb("row_idx", [P, UNROLL, 1], I32)
    sums = sb("sums", [P, UNROLL, D])
    cat_ps = [b[:, 0:P] for b in bank[0:UNROLL]]
    hid_ps = [b[:, P:2 * P] for b in bank[0:UNROLL]]
    dst_ps = [b[:, 2 * P:3 * P] for b in bank[0:UNROLL]]
    msg_ps = [b[:, 3 * P:3 * P + D] for b in bank[0:UNROLL]]
    sum_ps = [b[:, 3 * P + 64:3 * P + 64 + D] for b in bank[0:UNROLL]]
    xa, xsq = ([tile[:, 0:G * D].rearrange("p (g d) -> p g d", d=D) for tile in given[k]] for k in ("xa_in", "xsq_in"))
    mean = sb("mean", [P, LN_SLOTS, G])
    var = sb("var", [P, LN_SLOTS, G])
    std = sb("std", [P, LN_SLOTS, G])
    rstd = sb("rstd", [P, LN_SLOTS, G])

    idx_in = sem("idx_in")
    acc_start = sem("acc_start")
    consts = sem("consts")
    const_base = sem("const_base")
    dst_ready = sem("dst_ready")
    dst_placed = sem("dst_placed")
    may_gather = sem("may_gather")
    may_scatter = sem("may_scatter")
    idx_base = sem("idx_base")
    idx_paired = sem("idx_paired")
    idx_placed = sem("idx_placed")
    edge_in = [sem(f"edge_in{u}") for u in range(UNROLL)]
    xdst_in = [sem(f"xdst_in{u}") for u in range(UNROLL)]
    xsrc_in = [sem(f"xsrc_in{u}") for u in range(UNROLL)]
    cat_placed = sem("cat_placed")
    cat_copied = sem("cat_copied")
    hid_done = sem("hid_done")
    relu_done = sem("relu_done")
    msg_done = sem("msg_done")
    msg_copied = sem("msg_copied")
    dst_spread = sem("dst_spread")
    same_done = sem("same_done")
    step_done = sem("step_done")
    row_done = sem("row_done")
    sum_done = sem("sum_done")
    sum_copied = sem("sum_copied")
    scattered = sem("scattered")
    chunk_in = [sem(f"chunk_in{s}") for s in range(LN_SLOTS)]
    mean_done = sem("mean_done")
    centred = sem("centred")
    squared = sem("squared")
    var_done = sem("var_done")
    std_done = sem("std_done")
    rstd_done = sem("rstd_done")
    normed = sem("normed")
    ln_step = sem("ln_step")
    chunk_out = [sem(f"chunk_out{s}") for s in range(LN_SLOTS)]

    main = TILES * P
    src_v = src[0:main].rearrange("(p t) -> p t", p=P)
    dst_v = dst[0:main].rearrange("(p t) -> p t", p=P)
    edge_v = edge_attr[0:main, :].rearrange("(p t) d -> p t d", p=P)

    def rows(t):
        return TAIL if isinstance(t, int) and t == TILES else P

    def tiles(eng, step):
        for u in range(UNROLL):
            step(0, u)
        with eng.Fori(1, TROUNDS) as r:
            for u in range(UNROLL):
                step(r, u)
        step(TROUNDS, 0)

    def tile_of(r, u):
        return r * UNROLL + u

    def ln_rows(c):
        return P if c < CHUNKS else NREST

    def ln_cols(c):
        return G if c < CHUNKS else 1

    def ln_pair(c, table, tile):
        s = c % LN_SLOTS
        if c < CHUNKS:
            t = table[0:PER * P, :].rearrange("(p j) d -> p j d", p=P)[:, c * G:(c + 1) * G, :]
            return t, tile[s][:, :, :]
        return table[PER * P:N, :], tile[s][0:NREST, 0, :]

    def sync(sp):
        sp.dma_start(dst_idx[:, 0:TILES], dst_v).then_inc(idx_in, 16)
        sp.dma_start(src_idx[:, 0:TILES], src_v).then_inc(idx_in, 16)
        sp.dma_start(dst_idx[0:TAIL, TILES:TILES + 1], dst[main:E].rearrange("(p t) -> p t", t=1)).then_inc(idx_in, 16)
        sp.dma_start(src_idx[0:TAIL, TILES:TILES + 1], src[main:E].rearrange("(p t) -> p t", t=1)).then_inc(idx_in, 16)

        def load_edges(r, u):
            t = tile_of(r, u)
            n = rows(t)
            if not (isinstance(r, int) and r == 0):
                sp.wait_ge(cat_placed, t - UNROLL + 1)
            source = edge_attr[main:E, :] if n == TAIL else edge_v[:, bass.ds(t, 1), :].rearrange("p t d -> p (t d)")
            sp.dma_start(cat[0:n, u, 2 * D:P], source).then_inc(edge_in[u], 16)

        tiles(sp, load_edges)
        sp.wait_ge(scattered, 16 * (TILES + 1))
        for c in range(CHUNKS + 1):
            s = c % LN_SLOTS
            if c >= LN_SLOTS:
                sp.wait_ge(chunk_out[s], 16 * (c // LN_SLOTS))
            sp.dma_start(*ln_pair(c, acc, xa)[::-1]).then_inc(chunk_in[s], 16)

    def gpsimd(pool):
        pool.memset(lower[:, :], 1.0).then_inc(const_base, 1)
        pool.wait_ge(const_base, 1)
        pool.affine_select(out=lower[:, :], in_=lower[:, :], pattern=[[-1, P]], compare_op=ALU.is_gt,
                           fill=0.0, base=0, channel_multiplier=1).then_inc(consts, 1)
        pool.iota(spare_row_i[:, :], pattern=[[0, 1]], base=N, channel_multiplier=1).then_inc(consts, 1)

        def gather(r, u):
            t = tile_of(r, u)
            n = rows(t)
            if not (isinstance(r, int) and r == 0):
                pool.wait_ge(cat_placed, t - UNROLL + 1)
            pool.wait_ge(idx_placed, t + 1)
            pool.sem_inc(may_gather, 1)
            pool.indirect_dma_start(cat[0:n, u, 0:D], None, x[:, :],
                                    bass.IndirectOffsetOnAxis(ap=tile_idx[0:n, u, 0:1], axis=0)).then_inc(xdst_in[u], 16)
            pool.indirect_dma_start(cat[0:n, u, D:2 * D], None, x[:, :],
                                    bass.IndirectOffsetOnAxis(ap=tile_idx[0:n, u, 1:2], axis=0)).then_inc(xsrc_in[u], 16)

        def scatter(t, u):
            n = rows(t)
            pool.wait_ge(sum_copied, t + 1)
            pool.wait_ge(row_done, t + 1)
            if not (isinstance(t, int) and t == 0):
                pool.wait_ge(scattered, 16 * t)
            pool.sem_inc(may_scatter, 1)
            pool.indirect_dma_start(acc[:, :], bass.IndirectOffsetOnAxis(ap=row_idx[0:n, u, :], axis=0),
                                    sums[0:n, u, :], None, compute_op=ALU.add).then_inc(scattered, 16)

        for u in range(UNROLL):
            gather(0, u)
            if u == SCATTER_LAG:
                pool.wait_ge(acc_start, 32)
            if u >= SCATTER_LAG:
                scatter(u - SCATTER_LAG, u - SCATTER_LAG)
        with pool.Fori(1, TROUNDS) as r:
            for u in range(UNROLL):
                gather(r, u)
                scatter(tile_of(r, u) - SCATTER_LAG, (u - SCATTER_LAG) % UNROLL)
        gather(TROUNDS, 0)
        for t in range(TILES - SCATTER_LAG, TILES + 1):
            scatter(t, t % UNROLL)
        for c in range(CHUNKS + 1):
            s, n, g = c % LN_SLOTS, ln_rows(c), ln_cols(c)
            pool.wait_ge(rstd_done, c + 1)
            pool.tensor_tensor(xa[s][0:n, 0:g, :], xa[s][0:n, 0:g, :],
                               rstd[0:n, s, 0:g].unsqueeze(2).broadcast_to([n, g, D]), ALU.mult).then_inc(normed, 1)

    def tensor(pe):

        def step(r, u):
            t = tile_of(r, u)
            n = rows(t)
            first = isinstance(r, int) and r == 0
            if not first:
                pe.wait_ge(sum_copied, t - UNROLL + 1)
            pe.wait_ge(dst_placed, t + 1)
            pe.transpose(dst_ps[u][0:n, 0:n], tile_dst[0:n, u:u + 1].broadcast_to([n, n]),
                         ident[0:n, 0:n]).then_inc(dst_spread, 1)
            rr = 16 * (r + 1)
            pe.wait_ge(edge_in[u], rr)
            pe.wait_ge(xdst_in[u], rr)
            pe.wait_ge(xsrc_in[u], rr)
            pe.wait_ge(same_done, t + 1)
            pe.transpose(cat_ps[u][:, 0:n], cat[0:n, u, :], ident[0:n, 0:n]).then_inc(cat_placed, 1)
            pe.wait_ge(cat_copied, t + 1)
            pe.matmul(hid_ps[u][:, 0:n], w1[:, :], cat_t[:, u, 0:n], start=True, stop=True).then_inc(hid_done, 1)
            pe.wait_ge(relu_done, t + 1)
            pe.matmul(msg_ps[u][0:n, :], hid_t[:, u, 0:n], w2[:, :], start=True, stop=True).then_inc(msg_done, 1)
            pe.wait_ge(msg_copied, t + 1)
            pe.matmul(sum_ps[u][0:n, :], same[0:n, u, 0:n], msg[0:n, u, :], start=True, stop=True).then_inc(sum_done, 1)

        tiles(pe, step)

    def scalar(act):
        flat_x = x.rearrange("n d -> (n d)").rearrange("(k m) -> k m", k=3 * P)
        flat_a = acc[0:N, :].rearrange("n d -> (n d)").rearrange("(k m) -> k m", k=3 * P)
        act.dma_start(flat_a, flat_x).then_inc(acc_start, 16)
        act.dma_start(acc[N:N + P, :], x[0:P, :]).then_inc(acc_start, 16)
        act.wait_ge(idx_paired, 4)
        for t in range(UNROLL - 1):
            act.activation(tile_idx[:, t, :], node_idx[:, t, :], ACT.Copy).then_inc(idx_placed, 1)

        def step(r, u):
            t = tile_of(r, u)
            n = rows(t)
            act.wait_ge(cat_placed, t + 1)
            act.activation(cat_t[:, u, 0:n], cat_ps[u][:, 0:n], ACT.Copy).then_inc(cat_copied, 1)
            if not (isinstance(r, int) and r == TROUNDS):
                act.activation(tile_idx[:, (u - 1) % UNROLL, :],
                               node_idx[:, bass.ds(t + UNROLL - 1, 1), :].rearrange("p t k -> p (t k)"),
                               ACT.Copy).then_inc(idx_placed, 1)
            act.wait_ge(hid_done, t + 1)
            act.activation(hid_t[:, u, 0:n], hid_ps[u][:, 0:n], ACT.Relu, bias=b1c[:, 0:1]).then_inc(relu_done, 1)

        tiles(act, step)
        for c in range(CHUNKS + 2):
            if c <= CHUNKS:
                s, n, g = c % LN_SLOTS, ln_rows(c), ln_cols(c)
                act.wait_ge(centred, c + 1)
                if c >= LN_SLOTS:
                    act.wait_ge(var_done, c - LN_SLOTS + 1)
                act.activation(xsq[s][0:n, 0:g, :], xa[s][0:n, 0:g, :], ACT.Square).then_inc(squared, 1)
                act.wait_ge(var_done, c + 1)
                act.activation(std[0:n, s, 0:g], var[0:n, s, 0:g], ACT.Sqrt, bias=eps[0:n, 0:1],
                               scale=1.0 / D).then_inc(std_done, 1)
            if c >= 1:
                act.wait_ge(normed, c)
                act.dma_start(*ln_pair(c - 1, out, xa)).then_inc(chunk_out[(c - 1) % LN_SLOTS], 16)
        for s in range(LN_SLOTS):
            act.wait_ge(chunk_out[s], 16 * len(range(s, CHUNKS + 1, LN_SLOTS)))

    def vector(dve):
        dve.memset(node_idx[:, TILES:TILES + UNROLL, :], 0).then_inc(idx_base, 1)
        dve.wait_ge(idx_in, 64)
        dve.wait_ge(idx_base, 1)
        for k, idx in enumerate((dst_idx, src_idx)):
            dve.tensor_copy(node_idx[:, 0:TILES, k], idx[:, 0:TILES]).then_inc(idx_paired, 1)
            dve.tensor_copy(node_idx[0:TAIL, TILES, k:k + 1], idx[0:TAIL, TILES:TILES + 1]).then_inc(idx_paired, 1)
        dve.wait_ge(consts, 2)
        dve.tensor_copy(spare_row[:, :], spare_row_i[:, :]).then_inc(dst_ready, 1)
        dve.tensor_copy(dst_f[:, 0:TILES], dst_idx[:, 0:TILES]).then_inc(dst_ready, 1)
        dve.tensor_copy(dst_f[0:TAIL, TILES:TILES + 1], dst_idx[0:TAIL, TILES:TILES + 1]).then_inc(dst_ready, 1)
        dve.wait_ge(dst_ready, 3)
        dve.tensor_scalar(spare_less_dst[:, 0:TILES], dst_f[:, 0:TILES], -1.0, spare_row[:, 0:1],
                          ALU.mult, ALU.add).then_inc(dst_ready, 1)
        dve.tensor_scalar(spare_less_dst[0:TAIL, TILES:TILES + 1], dst_f[0:TAIL, TILES:TILES + 1], -1.0,
                          spare_row[0:TAIL, 0:1], ALU.mult, ALU.add).then_inc(dst_ready, 1)
        dve.wait_ge(dst_ready, 5)

        def step(r, u):
            t = tile_of(r, u)
            n = rows(t)
            dve.tensor_copy(tile_dst[0:n, u:u + 1], dst_f[0:n, bass.ds(t, 1)]).then_inc(dst_placed, 1)
            dve.wait_ge(dst_spread, t + 1)
            dve.tensor_scalar(same[0:n, u, 0:n], dst_ps[u][0:n, 0:n], tile_dst[0:n, u:u + 1], None,
                              ALU.is_equal).then_inc(same_done, 1)
            dve.wait_ge(same_done, t + 1)
            dve.tensor_tensor_reduce(earlier[0:n, u, 0:n], same[0:n, u, 0:n], lower[0:n, 0:n], 1.0, 0.0,
                                     ALU.mult, ALU.add, n_earlier[0:n, u:u + 1]).then_inc(step_done, 1)
            dve.wait_ge(step_done, 2 * t + 1)
            dve.tensor_scalar(repeated[0:n, u:u + 1], n_earlier[0:n, u:u + 1], 0.5, None,
                              ALU.is_ge).then_inc(step_done, 1)
            dve.wait_ge(step_done, 2 * t + 2)
            if not (isinstance(r, int) and r == 0):
                dve.wait_ge(scattered, 16 * (t - UNROLL + 1))
            dve.tensor_scalar(row_idx[0:n, u, :], spare_less_dst[0:n, bass.ds(t, 1)], repeated[0:n, u:u + 1],
                              tile_dst[0:n, u:u + 1], ALU.mult, ALU.add).then_inc(row_done, 1)
            dve.wait_ge(msg_done, t + 1)
            dve.tensor_tensor(msg[0:n, u, :], msg_ps[u][0:n, :], b2b[0:n, :], ALU.add).then_inc(msg_copied, 1)
            dve.wait_ge(sum_done, t + 1)
            dve.tensor_copy(sums[0:n, u, :], sum_ps[u][0:n, :]).then_inc(sum_copied, 1)

        tiles(dve, step)
        for c in range(CHUNKS + 1):
            s, n, g = c % LN_SLOTS, ln_rows(c), ln_cols(c)
            xc = xa[s][0:n, 0:g, :]
            dve.wait_ge(chunk_in[s], 16 * (c // LN_SLOTS + 1))
            if c >= LN_SLOTS:
                dve.wait_ge(std_done, c - LN_SLOTS + 1)
                dve.wait_ge(normed, c - LN_SLOTS + 1)
            dve.tensor_reduce(mean[0:n, s, 0:g], xc, AX_X, ALU.add).then_inc(ln_step, 1)
            dve.wait_ge(ln_step, 2 * c + 1)
            dve.tensor_scalar(mean[0:n, s, 0:g], mean[0:n, s, 0:g], 1.0 / D, None, ALU.mult).then_inc(ln_step, 1)
            dve.wait_ge(ln_step, 2 * c + 2)
            dve.tensor_tensor(xc, xc, mean[0:n, s, 0:g].unsqueeze(2).broadcast_to([n, g, D]),
                              ALU.subtract).then_inc(centred, 1)
            dve.wait_ge(squared, c + 1)
            dve.tensor_reduce(var[0:n, s, 0:g], xsq[s][0:n, 0:g, :], AX_X, ALU.add).then_inc(var_done, 1)
            dve.wait_ge(std_done, c + 1)
            dve.reciprocal(rstd[0:n, s, 0:g], std[0:n, s, 0:g]).then_inc(rstd_done, 1)

    return {"sync": sync, "gpsimd": gpsimd, "tensor": tensor, "scalar": scalar, "vector": vector}


def gnn_resnorm_kernel(nc, x, src, dst, edge_attr, W1, b1, W2, b2, out):
    N, D = x.shape
    E, DE = edge_attr.shape
    FIN, HID = W1.shape
    assert FIN == P and HID == P and 2 * D + DE == P

    FULL = N // BLOCK
    REST = N - FULL * BLOCK
    NB = FULL + 1
    RJ = 2
    RP = REST // RJ
    assert RP * RJ == REST and RP <= P and 0 < FULL % SUPER
    FULL_SUPERS = FULL // SUPER
    NS = FULL_SUPERS + 2
    ROUNDS = (FULL_SUPERS - AHEAD) // BODY
    SD = SUPER * J * D
    EC = -(-E // P)
    EP = E // EC
    EREST = E - EP * EC
    assert EP == P - 1 and 0 < EREST < EC
    EK = EP // 16 * 16
    PAD_P = P - 32
    TCH = 4
    TC = EC // TCH
    assert TC * TCH == EC
    PAD_PART = EREST // TC
    ROWS = P * EC
    LAST = ROWS - P
    assert LAST + P >= E
    FAR = 1 << 20
    BG = 100
    NG = 3
    assert NG * BG >= NB + 1 and N < FAR

    edge_table = nc.dram_tensor("edge_table", (ROWS, DE + META), F32, kind="Internal").ap()
    acc = nc.dram_tensor("acc", (N + P, D), F32, kind="Internal").ap()

    with ExitStack() as ctx:
        def sb(name, shape, dt=F32):
            return ctx.enter_context(nc.sbuf_tensor(name, shape, dt))

        def sem(name):
            return ctx.enter_context(nc.semaphore(name))

        bank = [ctx.enter_context(nc.psum_tensor(f"bank{i}", [P, 512], F32)) for i in range(8)]

        ident = sb("ident", [P, P])
        ones = sb("ones", [P, P])
        w1 = sb("w1", [P, HID])
        b1c = sb("b1c", [HID, 1])
        w2 = sb("w2", [HID, D])
        b2b = sb("b2b", [P, D])
        eps = sb("eps", [P, 1])

        dst_pm = sb("dst_pm", [P, EC], I32)
        src_pm = sb("src_pm", [P, EC], I32)
        edge_pm = sb("edge_pm", [P, EC, DE])
        table_pm = sb("table_pm", [P, EC, DE + META])
        dst_rows = sb("dst_rows", [P, EC + 1])
        first_dst = sb("first_dst", [P, 1])
        next_dst_i = sb("next_dst_i", [P, 1], I32)
        next_dst = sb("next_dst", [P, 1])
        int_row = sb("int_row", [P, NG * BG], I32)
        bound_row = sb("bound_row", [P, NG * BG])
        int_col = sb("int_col", [P, 2], I32)
        bound_col = sb("bound_col", [P, NG])
        past_next = sb("past_next", [P, NG * BG])
        holder = sb("holder", [P, NG * BG])
        below = sb("below", [P, NG, EC])
        n_below = sb("n_below", [P, NG])
        first_col = sb("first_col", [P, NG])
        first_row = sb("first_row", [1, NG * BG])
        first_clamped = sb("first_clamped", [1, NG * BG])
        first_edge = sb("first_edge", [1, NG * BG // SUPER * 4], I32)
        counts = sb("counts", [1, NG * BG])
        most = sb("most", [1, 1])
        crowded = sb("crowded", [1, 1])
        falls = sb("falls", [P, EC])
        unsorted = sb("unsorted", [P, 1])
        general_f = sb("general_f", [1, 1])
        general = sb("general", [1, 1], I32)

        ident_b = sb("ident_b", [P, P], BF16)
        node_of_i = sb("node_of_i", [P, BLOCK], I32)
        node_of = sb("node_of", [P, BLOCK], F16)
        short_node_of = sb("short_node_of", [P, REST], F16)
        block_start = sb("block_start", [P, NB])
        block_start_i = sb("block_start_i", [P, NB], I32)
        ones_b = sb("ones_b", [P, P], BF16)
        b2_rest = sb("b2_rest", [P, D])
        b2_low = sb("b2_low", [P, D])
        b2_rows = sb("b2_rows", [P, D])
        b2_parts = sb("b2_parts", [P, SUPER, D], BF16)
        dst_in_block = sb("dst_in_block", [P, SMALL, SUPER])
        cat = sb("cat", [P, BODY, SUPER, P + META])
        onehot = sb("onehot", [P, BODY, SUPER, BLOCK], BF16)
        onehot_t = sb("onehot_t", [P, SMALL, SUPER, J * P], BF16)
        cat_t = sb("cat_t", [P, SMALL, SUPER * P])
        hid_t = sb("hid_t", [P, SMALL, SUPER * P])
        msg = sb("msg", [P, SMALL, SUPER * D])
        msg_rest = sb("msg_rest", [P, SMALL, SUPER * D])
        msg_low = sb("msg_low", [P, SMALL, SUPER * D], BF16)
        xs = sb("xs", [P, BODY, SD])
        x_rest = sb("x_rest", [P, BODY, SD])
        x_low = sb("x_low", [P, BODY, SD], BF16)
        ys = sb("ys", [P, BODY, SD])
        sq = sb("sq", [P, SMALL, SD])
        total = sb("total", [P, SMALL, SUPER * J])
        sq_total = sb("sq_total", [P, SMALL, SUPER * J])
        std = sb("std", [P, SMALL, SUPER * J])
        rstd = sb("rstd", [P, SMALL, SUPER * J])
        onehot_ps = [bank[i][:, :].bitcast(BF16) for i in range(2)]
        cat_ps, hid_ps, xdst_ps, msg_ps = bank[2], bank[3], bank[4], bank[5]
        sum_ps = bank[6:8]

        const_base = sem("const_base")
        consts = sem("consts")
        weights_in = sem("weights_in")
        pad_set = sem("pad_set")
        dst_in = sem("dst_in")
        src_in = sem("src_in")
        next_in = sem("next_in")
        attr_in = [sem(f"attr_in{c}") for c in range(TCH)]
        attr_rest_in = sem("attr_rest_in")
        setup = sem("setup")
        cols_placed = sem("cols_placed")
        attr_placed = sem("attr_placed")
        table_out = sem("table_out")
        holder_ready = sem("holder_ready")
        rows_ready = sem("rows_ready")
        first_ready = sem("first_ready")
        first_turned = sem("first_turned")
        fell_ready = sem("fell_ready")
        fell_summed = sem("fell_summed")
        first_done = sem("first_done")
        general_done = sem("general_done")
        b2_ready = sem("b2_ready")
        row_in = [sem(f"row_in{s}") for s in range(BODY)]
        xsrc_in = [sem(f"xsrc_in{s}") for s in range(BODY)]
        x_in = [sem(f"x_in{s}") for s in range(BODY)]
        y_out = [sem(f"y_out{s}") for s in range(BODY)]
        may_gather = sem("may_gather")
        onehot_ready = sem("onehot_ready")
        onehot_turned = sem("onehot_turned")
        onehot_t_ready = sem("onehot_t_ready")
        xdst_done = sem("xdst_done")
        xdst_placed = sem("xdst_placed")
        cat_turned = sem("cat_turned")
        cat_t_ready = sem("cat_t_ready")
        hid_done = sem("hid_done")
        hid_t_ready = sem("hid_t_ready")
        msg_done = sem("msg_done")
        msg_ready = sem("msg_ready")
        msg_rest_ready = sem("msg_rest_ready")
        msg_split = sem("msg_split")
        x_rest_ready = sem("x_rest_ready")
        x_split = sem("x_split")
        dst_counted = sem("dst_counted")
        sum_done = sem("sum_done")
        totalled = sem("totalled")
        centred = sem("centred")
        squared = sem("squared")
        sq_totalled = sem("sq_totalled")
        std_ready = sem("std_ready")
        rstd_ready = sem("rstd_ready")
        normed = sem("normed")

        def load_attributes(eng, c):
            attr_v = edge_attr[0:EP * EC, :].rearrange("(p t) d -> p t d", p=EP)
            for p0, p1 in ((0, EK), (EK, EP)):
                eng.dma_start(edge_pm[p0:p1, c * TC:(c + 1) * TC, :], attr_v[p0:p1, c * TC:(c + 1) * TC, :]).then_inc(attr_in[c], 16)

        def exists(g):
            return not isinstance(g, int) or 0 <= g < NS

        def after(g, k):
            return not isinstance(g, int) or g >= k

        def shape_of(g):
            if isinstance(g, int) and g == NS - 1:
                return RP, 1, RJ
            return BP, FULL % SUPER if isinstance(g, int) and g == NS - 2 else SUPER, J

        def first_block(g):
            return FULL if isinstance(g, int) and g == NS - 1 else g * SUPER

        def super_row(g):
            return FULL // SUPER if isinstance(g, int) and g == NS - 1 else g

        def first_place(g):
            return FULL % SUPER if isinstance(g, int) and g == NS - 1 else 0

        def walk(eng, stages):
            def run(stage, q, v):
                g = q * BODY + v
                if exists(g):
                    stage(g, q, v)

            for t in range(min(k for k, stage in stages), PEELED * BODY):
                for k, stage in stages:
                    run(stage, *divmod(t - k, BODY))
            with eng.Fori(PEELED, ROUNDS) as r:
                for u in range(BODY):
                    for k, stage in stages:
                        q, v = divmod(u - k, BODY)
                        run(stage, r + q, v)
            for t in range(ROUNDS * BODY, NS + max(k for k, stage in stages)):
                for k, stage in stages:
                    run(stage, *divmod(t - k, BODY))

        def dram_rows(table, g):
            n, blocks, jj = shape_of(g)
            if jj == RJ:
                return table[FULL * BLOCK:N, :].rearrange("(p j) d -> p (j d)", j=RJ)
            return table[0:FULL * BLOCK, :].rearrange("(b p j) d -> p b (j d)", p=BP, j=J)[:, bass.ds(g * SUPER, blocks), :]

        def sbuf_rows(tile, g, s):
            n, blocks, jj = shape_of(g)
            flat = tile[0:n, s, 0:blocks * jj * D]
            return flat if jj == RJ else flat.rearrange("p (b m) -> p b m", b=blocks)

        def flat_of(tile, g, s):
            n, blocks, jj = shape_of(g)
            return tile[0:n, s, 0:blocks * jj * D]

        def upper_half(tile):
            return tile.bitcast(BF16)[:, 1::2]

        def by_node(tile, g, s):
            return flat_of(tile, g, s).rearrange("p (m d) -> p m d", d=D)

        general_engine = general_path(nc, ctx, dict(
            x=x, src=src, dst=dst, edge_attr=edge_attr, out=out, acc=acc, w1=w1, w2=w2, b1c=b1c, b2b=b2b,
            ident=ident, eps=eps, bank=bank,
            xa_in=[onehot[:, :, :, :].rearrange("p s b n -> p (s b n)").bitcast(F32), xs[:, :, :].rearrange("p s m -> p (s m)")],
            xsq_in=[t[:, :, :].rearrange("p t c -> p (t c)") for t in (edge_pm, table_pm)],
            general=general, general_done=general_done))
        block = ctx.enter_context(nc.Block())

        @block.sync
        def _(sp):
            tables = (dst, dst_pm, dst_in), (src, src_pm, src_in)
            for table, idx, done in tables:
                full = table[0:EP * EC].rearrange("(p t) -> p t", p=EP)
                sp.dma_start(idx[0:PAD_P, :], full[0:PAD_P, :]).then_inc(done, 16)
                sp.wait_ge(pad_set, 3)
                sp.dma_start(idx[PAD_P:EP, :], full[PAD_P:EP, :]).then_inc(done, 16)
                sp.dma_start(idx[EP:P, 0:EREST], table[EP * EC:E].rearrange("(a t) -> a t", a=1)).then_inc(done, 16)
                if table is dst:
                    sp.dma_start(next_dst_i[0:EP, :], dst[EC:E].rearrange("(p t) -> p t", t=1)[0:(EP - 1) * EC + 1:EC, :],
                                 allow_slow_non_contiguous=True).then_inc(next_in, 16)
            sp.wait_ge(pad_set, 4)
            for c in range(PAD_PART, TCH):
                load_attributes(sp, c)
            sp.dma_start(w1[:, :], W1).then_inc(weights_in, 16)
            sp.dma_start(w2[:, :], W2).then_inc(weights_in, 16)
            sp.dma_start(b1c[:, :], b1.rearrange("(p t) -> p t", t=1)).then_inc(weights_in, 16)
            sp.dma_start(b2b[:, :], b2.rearrange("(a d) -> a d", a=1).broadcast_to([P, D])).then_inc(weights_in, 16)
            sp.wait_ge(cols_placed, 2)
            for c in range(TCH):
                sp.wait_ge(attr_placed, c + 1)
                sp.dma_start(edge_table.rearrange("(p t) c -> p t c", p=P)[:, c * TC:(c + 1) * TC, :].rearrange("p t c -> p (t c)"),
                             table_pm[:, c * TC:(c + 1) * TC, :].rearrange("p t c -> p (t c)")).then_inc(table_out, 16)
            sp.wait_ge(first_done, 1)
            sp.wait_ge(table_out, 16 * TCH)

            def numbers(row):
                return nc.values_load_multi_w_load_instructions(row, engines=[mybir.EngineType.SP], min_val=0, max_val=LAST)[1]

            def load_edges(g, r, v):
                n, blocks, jj = shape_of(g)
                if after(g, BODY):
                    sp.wait_ge(cat_turned, g - BODY + 1)
                firsts = numbers(first_edge[0:1, bass.ds(super_row(g) * 4, SUPER)])
                for k in range(SUPER):
                    first = firsts[first_place(g) + min(k, blocks - 1)]
                    sp.dma_start(cat[:, v, k, 2 * D:P + META], edge_table[bass.ds(first, P), :]).then_inc(row_in[v], 16)

            def load_nodes(g, r, v):
                if after(g, BODY):
                    sp.wait_ge(sum_done, g - BODY + 1)
                sp.dma_start(sbuf_rows(xs, g, v), dram_rows(x, g)).then_inc(x_in[v], 16)

            def store(g, r, v):
                sp.wait_ge(normed, g + 1)
                sp.dma_start(dram_rows(out, g), sbuf_rows(ys, g, v)).then_inc(y_out[v], 16)

            walk(sp, ((-AHEAD, load_edges), (-X_AHEAD, load_nodes), (9, store)))
            for s in range(BODY):
                sp.wait_ge(y_out[s], 16 * len(range(s, NS, BODY)))
            sp.wait_ge(general_done, 1)
            needed = sp.value_load(general[0:1, 0:1], min_val=0, max_val=1)
            with sp.If(needed > 0):
                general_engine["sync"](sp)

        @block.gpsimd
        def _(pool):
            pool.memset(ident[:, :], 0.0).then_inc(const_base, 1)
            pool.iota(int_row[:, :], pattern=[[BLOCK, NG * BG]], base=0, channel_multiplier=0).then_inc(consts, 1)
            pool.iota(int_col[:, 0:1], pattern=[[0, 1]], base=0, channel_multiplier=BLOCK).then_inc(consts, 1)
            pool.iota(int_col[:, 1:2], pattern=[[0, 1]], base=0, channel_multiplier=EC).then_inc(consts, 1)
            pool.iota(node_of_i[:, :], pattern=[[1, J], [J, BP]], base=0, channel_multiplier=0).then_inc(consts, 1)
            pool.wait_ge(const_base, 1)
            pool.affine_select(out=ident[:, :], in_=ident[:, :], pattern=[[-1, P]], compare_op=ALU.not_equal,
                               fill=1.0, base=0, channel_multiplier=1).then_inc(consts, 1)
            pool.wait_ge(setup, 1)
            pool.iota(node_of_i[:, 0:REST], pattern=[[1, RJ], [RJ, RP]], base=0, channel_multiplier=0).then_inc(consts, 1)
            pool.iota(block_start_i[:, :], pattern=[[BLOCK, NB]], base=0, channel_multiplier=0).then_inc(consts, 1)
            pool.wait_ge(src_in, 48)
            pool.tensor_copy(table_pm[:, :, DE + 1].bitcast(I32), src_pm[:, :]).then_inc(cols_placed, 1)

            def gather_xsrc(g, r, v):
                pool.wait_ge(row_in[v], 16 * SUPER * (r + 1))
                pool.sem_inc(may_gather, 1)
                for k in range(SUPER):
                    pool.indirect_dma_start(cat[:, v, k, D:2 * D], None, x[:, :], bass.IndirectOffsetOnAxis(
                        ap=cat[:, v, k, P + 1:P + 2].bitcast(I32), axis=0)).then_inc(xsrc_in[v], 16)

            def scale(g, r, v):
                n, blocks, jj = shape_of(g)
                y = by_node(ys, g, v)
                pool.wait_ge(rstd_ready, g + 1)
                pool.tensor_tensor(y, y, rstd[0:n, v % SMALL, 0:blocks * jj].unsqueeze(2).broadcast_to([n, blocks * jj, D]),
                                   ALU.mult).then_inc(normed, 1)

            walk(pool, ((1 - AHEAD, gather_xsrc), (8, scale)))
            pool.wait_ge(general_done, 1)
            needed = pool.value_load(general[0:1, 0:1], min_val=0, max_val=1)
            with pool.If(needed > 0):
                general_engine["gpsimd"](pool)

        @block.tensor
        def _(pe):
            pe.wait_ge(consts, 5)
            pe.wait_ge(holder_ready, 1)
            for i in range(NG):
                pe.matmul(bank[i][0:BG, 0:EC + 1], holder[:, i * BG:(i + 1) * BG], dst_rows[:, :],
                          start=True, stop=True).then_inc(rows_ready, 1)
            pe.wait_ge(fell_ready, 1)
            pe.matmul(bank[3][0:1, 0:1], unsorted[:, :], ones[:, 0:1], start=True, stop=True).then_inc(fell_summed, 1)
            pe.wait_ge(first_ready, NG)
            for i in range(NG):
                pe.transpose(bank[4][0:1, i * BG:(i + 1) * BG], first_col[0:BG, i:i + 1],
                             ident[0:BG, 0:BG]).then_inc(first_turned, 1)
            pe.wait_ge(weights_in, 64)
            pe.wait_ge(general_done, 1)
            pe.wait_ge(b2_ready, 1)

            def turn_cat(g, r, v):
                n, blocks, jj = shape_of(g)
                pe.wait_ge(xdst_placed, g + 1)
                pe.wait_ge(xsrc_in[v], 16 * SUPER * (r + 1))
                for k in range(blocks):
                    last = pe.transpose(cat_ps[:, k * P:(k + 1) * P], cat[:, v, k, 0:P], ident[:, :])
                last.then_inc(cat_turned, 1)

            def turn_block(g, v, k):
                n, blocks, jj = shape_of(g)
                for j in range(jj):
                    last = pe.transpose(onehot_ps[k % 2][0:n, j * P:(j + 1) * P], onehot[:, v, k, j * n:(j + 1) * n],
                                        ident_b[:, :])
                last.then_inc(onehot_turned, 1)

            def turn_onehots(g, r, v):
                n, blocks, jj = shape_of(g)
                pe.wait_ge(onehot_ready, g + 1)
                if after(g, 1):
                    pe.wait_ge(onehot_t_ready, first_block(g))
                for k in range(min(blocks, 2)):
                    turn_block(g, v, k)

            def turn_last_onehot(g, r, v):
                n, blocks, jj = shape_of(g)
                if blocks == SUPER:
                    pe.wait_ge(onehot_t_ready, first_block(g) + 1)
                    turn_block(g, v, 2)

            def add_nodes(g, v, i):
                n, blocks, jj = shape_of(g)
                part = (upper_half(flat_of(xs, g, v)), upper_half(flat_of(x_rest, g, v)), flat_of(x_low, g, v))[i]
                if i == 0 and after(g, SMALL):
                    pe.wait_ge(centred, g - SMALL + 1)
                pe.matmul(sum_ps[v % SMALL][0:n, 0:blocks * jj * D], ident_b[0:n, 0:n], part, start=(i == 0), stop=False)

            def sums(g, r, v):
                n, blocks, jj = shape_of(g)
                ps, t, m = sum_ps[v % SMALL], v % SMALL, slice(0, blocks * D)
                msg_parts = upper_half(msg[:, t, m]), upper_half(msg_rest[:, t, m]), msg_low[:, t, m]
                pe.wait_ge(msg_split, g + 1)
                if isinstance(g, int) and g == NS - 1:
                    for i in range(PARTS):
                        add_nodes(g, v, i)
                for k in range(blocks):
                    for j in range(jj):
                        for i, part in enumerate(msg_parts):
                            last = pe.matmul(ps[0:n, (k * jj + j) * D:(k * jj + j + 1) * D], onehot[:, v, k, j * n:(j + 1) * n],
                                             part[:, k * D:(k + 1) * D], start=False,
                                             stop=(k == blocks - 1 and j == jj - 1 and i == PARTS - 1))
                last.then_inc(sum_done, 1)

            def hidden(g, r, v):
                n, blocks, jj = shape_of(g)
                pe.wait_ge(cat_t_ready, g + 1)
                pe.matmul(hid_ps[:, 0:blocks * P], w1[:, :], cat_t[:, v % SMALL, 0:blocks * P],
                          start=True, stop=True).then_inc(hid_done, 1)

            def fetch_xdst(g, r, v):
                n, blocks, jj = shape_of(g)
                parts = upper_half(flat_of(xs, g, v)), upper_half(flat_of(x_rest, g, v)), flat_of(x_low, g, v)
                pe.wait_ge(x_split, g + 1)
                pe.wait_ge(onehot_t_ready, first_block(g) + blocks)
                for k in range(blocks):
                    for j in range(jj):
                        for i, part in enumerate(parts):
                            last = pe.matmul(xdst_ps[:, k * D:(k + 1) * D], onehot_t[0:n, v % SMALL, k, j * P:(j + 1) * P],
                                             part[:, (k * jj + j) * D:(k * jj + j + 1) * D],
                                             start=(j == 0 and i == 0), stop=(j == jj - 1 and i == PARTS - 1))
                last.then_inc(xdst_done, 1)

            def messages(g, r, v):
                n, blocks, jj = shape_of(g)
                pe.wait_ge(hid_t_ready, g + 1)
                if after(g, 1):
                    pe.wait_ge(msg_ready, g)
                pe.matmul(msg_ps[:, 0:blocks * D], ones_b[:, :], b2_parts[:, 0:blocks, :].rearrange("p b d -> p (b d)"),
                          start=True, stop=False)
                for k in range(SUPER):
                    if after(g, 1):
                        add_nodes(g - 1, (v - 1) % BODY, k)
                    if k >= blocks:
                        continue
                    last = pe.matmul(msg_ps[:, k * D:(k + 1) * D], hid_t[:, v % SMALL, k * P:(k + 1) * P], w2[:, :],
                                     start=False, stop=(k == blocks - 1))
                    if k == blocks - 1:
                        last.then_inc(msg_done, 1)

            walk(pe, ((2, turn_cat), (0, turn_onehots), (5, sums), (2, hidden), (0, turn_last_onehot), (1, fetch_xdst),
                      (3, messages)))
            pe.wait_ge(general_done, 1)
            needed = pe.value_load(general[0:1, 0:1], min_val=0, max_val=1)
            with pe.If(needed > 0):
                general_engine["tensor"](pe)

        @block.scalar
        def _(act):
            act.dma_start(edge_pm[EP:P, 0:EREST, :], edge_attr[EP * EC:E, :].rearrange("(a t) d -> a t d", a=1)).then_inc(attr_rest_in, 16)
            for c in range(PAD_PART):
                load_attributes(act, c)
            for c in range(TCH):
                if c == 0:
                    act.wait_ge(attr_rest_in, 16)
                act.wait_ge(attr_in[c], 32)
                act.activation(table_pm[:, c * TC:(c + 1) * TC, 0:DE], edge_pm[:, c * TC:(c + 1) * TC, :],
                               ACT.Copy).then_inc(attr_placed, 1)
            act.wait_ge(weights_in, 64)

            def copy_cat(g, r, v):
                n, blocks, jj = shape_of(g)
                act.wait_ge(cat_turned, g + 1)
                act.activation(cat_t[:, v % SMALL, 0:blocks * P], cat_ps[:, 0:blocks * P], ACT.Copy).then_inc(cat_t_ready, 1)

            def copy_msg(g, r, v):
                n, blocks, jj = shape_of(g)
                act.wait_ge(msg_done, g + 1)
                if after(g, SMALL):
                    act.wait_ge(sum_done, g - SMALL + 1)
                act.activation(msg[:, v % SMALL, 0:blocks * D], msg_ps[:, 0:blocks * D], ACT.Copy).then_inc(msg_ready, 1)

            def copy_block(g, v, k):
                n, blocks, jj = shape_of(g)
                act.wait_ge(onehot_turned, first_block(g) + k + 1)
                act.activation(onehot_t[0:n, v % SMALL, k, 0:jj * P], onehot_ps[k % 2][0:n, 0:jj * P],
                               ACT.Copy).then_inc(onehot_t_ready, 1)

            def copy_onehots(g, r, v):
                n, blocks, jj = shape_of(g)
                for k in range(min(blocks, 2)):
                    copy_block(g, v, k)

            def copy_last_onehot(g, r, v):
                n, blocks, jj = shape_of(g)
                if blocks == SUPER:
                    copy_block(g, v, 2)

            def relu(g, r, v):
                n, blocks, jj = shape_of(g)
                act.wait_ge(hid_done, g + 1)
                act.activation(hid_t[:, v % SMALL, 0:blocks * P], hid_ps[:, 0:blocks * P], ACT.Relu,
                               bias=b1c[:, 0:1]).then_inc(hid_t_ready, 1)

            def place_xdst(g, r, v):
                n, blocks, jj = shape_of(g)
                act.wait_ge(xdst_done, g + 1)
                act.activation(cat[:, v, 0:blocks, 0:D], xdst_ps[:, 0:blocks * D].rearrange("p (b d) -> p b d", d=D),
                               ACT.Copy).then_inc(xdst_placed, 1)

            def square(g, r, v):
                act.wait_ge(centred, g + 1)
                act.activation(flat_of(sq, g, v % SMALL), flat_of(ys, g, v), ACT.Square).then_inc(squared, 1)

            def root(g, r, v):
                n, blocks, jj = shape_of(g)
                act.wait_ge(sq_totalled, g + 1)
                act.activation(std[0:n, v % SMALL, 0:blocks * jj], sq_total[0:n, v % SMALL, 0:blocks * jj], ACT.Sqrt,
                               bias=eps[0:n, 0:1], scale=1.0 / D).then_inc(std_ready, 1)

            walk(act, ((7, root), (2, copy_cat), (4, copy_msg), (0, copy_onehots), (6, square), (0, copy_last_onehot), (2, relu),
                       (1, place_xdst)))
            act.wait_ge(general_done, 1)
            needed = act.value_load(general[0:1, 0:1], min_val=0, max_val=1)
            with act.If(needed > 0):
                general_engine["scalar"](act)

        @block.vector
        def _(dve):
            n_setup = [0]

            def note(ins):
                n_setup[0] += 1
                ins.then_inc(setup, 1)
                dve.wait_ge(setup, n_setup[0])

            dve.memset(dst_pm[PAD_P:P, :], FAR).then_inc(pad_set, 1)
            dve.memset(next_dst_i[:, :], FAR).then_inc(pad_set, 1)
            dve.memset(src_pm[PAD_P:P, :], 0).then_inc(pad_set, 1)
            dve.memset(edge_pm[PAD_P:P, EREST:EC, :], 0.0).then_inc(pad_set, 1)
            dve.wait_ge(consts, 4)
            note(dve.tensor_copy(node_of[:, :], node_of_i[:, :]))
            dve.wait_ge(consts, 5)
            note(dve.tensor_copy(ident_b[:, :], ident[:, :]))
            note(dve.memset(ones[:, :], 1.0))
            note(dve.memset(eps[:, :], EPS))
            note(dve.tensor_copy(bound_row[:, :], int_row[:, :]))
            note(dve.tensor_copy(dst_rows[:, EC:EC + 1], int_col[:, 1:2]))
            for i in range(NG):
                note(dve.tensor_scalar(bound_col[:, i:i + 1], int_col[:, 0:1], float(i * BG * BLOCK), None, ALU.add))
            dve.wait_ge(dst_in, 48)
            note(dve.tensor_copy(dst_rows[:, 0:EC], dst_pm[:, :]))
            dve.wait_ge(next_in, 16)
            note(dve.tensor_copy(next_dst[:, :], next_dst_i[:, :]))
            note(dve.tensor_copy(first_dst[:, :], dst_rows[:, 0:1]))
            note(dve.memset(first_dst[0:1, :], -1.0))
            note(dve.tensor_scalar(past_next[:, :], bound_row[:, :], next_dst[:, 0:1], None, ALU.is_gt))
            dve.scalar_tensor_tensor(out=holder[:, :], in0=bound_row[:, :], scalar=first_dst[:, 0:1], in1=past_next[:, :],
                                     op0=ALU.is_gt, op1=ALU.subtract).then_inc(holder_ready, 1)
            dve.tensor_copy(table_pm[:, :, DE], dst_rows[:, 0:EC]).then_inc(cols_placed, 1)
            note(dve.tensor_tensor(falls[:, 0:EC - 1], dst_rows[:, 0:EC - 1], dst_rows[:, 1:EC], ALU.is_gt))
            note(dve.tensor_tensor(falls[:, EC - 1:EC], dst_rows[:, EC - 1:EC], next_dst[:, :], ALU.is_gt))
            dve.tensor_reduce(unsorted[:, :], falls[:, :], AX_X, ALU.add).then_inc(fell_ready, 1)
            for i in range(NG):
                dve.wait_ge(rows_ready, i + 1)
                note(dve.tensor_scalar(below[0:BG, i, :], bank[i][0:BG, 0:EC], bound_col[0:BG, i:i + 1], None, ALU.is_lt))
                note(dve.tensor_reduce(n_below[0:BG, i:i + 1], below[0:BG, i, :], AX_X, ALU.add))
                dve.tensor_tensor(first_col[0:BG, i:i + 1], bank[i][0:BG, EC:EC + 1], n_below[0:BG, i:i + 1],
                                  ALU.add).then_inc(first_ready, 1)
            dve.wait_ge(first_turned, NG)
            note(dve.tensor_copy(first_row[:, :], bank[4][0:1, 0:NG * BG]))
            note(dve.tensor_scalar(first_clamped[:, :], first_row[:, :], 0.0, float(LAST), ALU.max, ALU.min))
            note(dve.memset(first_edge[:, :], 0))
            dve.tensor_copy(first_edge[:, :].rearrange("a (g k) -> a g k", k=4)[:, :, 0:SUPER],
                            first_clamped[:, :].rearrange("a (g k) -> a g k", k=SUPER)).then_inc(first_done, 1)
            note(dve.tensor_tensor(counts[:, 0:NB], first_row[:, 1:NB + 1], first_row[:, 0:NB], ALU.subtract))
            note(dve.tensor_reduce(most[:, :], counts[:, 0:NB], AX_X, ALU.max))
            note(dve.tensor_scalar(crowded[:, :], most[:, :], P + 0.5, None, ALU.is_gt))
            dve.wait_ge(fell_summed, 1)
            note(dve.tensor_tensor(general_f[:, :], bank[3][0:1, 0:1], crowded[:, :], ALU.add))
            dve.tensor_scalar(general[:, :], general_f[:, :], 0.5, None, ALU.is_gt).then_inc(general_done, 1)
            dve.wait_ge(consts, 7)
            note(dve.tensor_copy(short_node_of[:, :], node_of_i[:, 0:REST]))
            note(dve.tensor_copy(block_start[:, :], block_start_i[:, :]))
            dve.wait_ge(weights_in, 64)
            note(dve.memset(ones_b[:, :], 1.0))
            note(dve.tensor_tensor(b2_rest[:, :], b2b[:, :], upper_half(b2b[:, :]), ALU.subtract))
            note(dve.tensor_tensor(b2_low[:, :], b2_rest[:, :], upper_half(b2_rest[:, :]), ALU.subtract))
            note(dve.tensor_scalar(b2_rows[:, :], upper_half(b2b[:, :]), ident[:, 0:1], None, ALU.mult))
            for i, part in ((1, upper_half(b2_rest[:, :])), (2, b2_low[:, :])):
                note(dve.scalar_tensor_tensor(out=b2_rows[:, :], in0=part, scalar=ident[:, i:i + 1], in1=b2_rows[:, :],
                                              op0=ALU.mult, op1=ALU.add))
            for k in range(1, SUPER):
                note(dve.tensor_copy(b2_parts[:, k, :], b2_rows[:, :]))
            dve.tensor_copy(b2_parts[:, 0, :], b2_rows[:, :]).then_inc(b2_ready, 1)

            def sums_of(g, t):
                n, blocks, jj = shape_of(g)
                return sum_ps[t][0:n, 0:blocks * jj * D].rearrange("p (m d) -> p m d", d=D)

            def total_sum(g, r, v):
                n, blocks, jj = shape_of(g)
                dve.wait_ge(sum_done, g + 1)
                dve.tensor_reduce(total[0:n, v % SMALL, 0:blocks * jj], sums_of(g, v % SMALL), AX_X, ALU.add).then_inc(totalled, 1)

            def centre(g, r, v):
                n, blocks, jj = shape_of(g)
                t, m = v % SMALL, blocks * jj
                dve.wait_ge(totalled, g + 1)
                if after(g, BODY):
                    dve.wait_ge(y_out[v], 16 * r)
                dve.scalar_tensor_tensor(out=by_node(ys, g, v), in0=total[0:n, t, 0:m].unsqueeze(2).broadcast_to([n, m, D]),
                                         scalar=-1.0 / D, in1=sums_of(g, t), op0=ALU.mult, op1=ALU.add).then_inc(centred, 1)

            def less_high_msg(g, r, v):
                n, blocks, jj = shape_of(g)
                t, w = v % SMALL, blocks * D
                dve.wait_ge(msg_ready, g + 1)
                dve.tensor_tensor(msg_rest[:, t, 0:w], msg[:, t, 0:w], upper_half(msg[:, t, 0:w]),
                                  ALU.subtract).then_inc(msg_rest_ready, 1)

            def less_middle_msg(g, r, v):
                n, blocks, jj = shape_of(g)
                t, w = v % SMALL, blocks * D
                dve.wait_ge(msg_rest_ready, g + 1)
                dve.tensor_tensor(msg_low[:, t, 0:w], msg_rest[:, t, 0:w], upper_half(msg_rest[:, t, 0:w]),
                                  ALU.subtract).then_inc(msg_split, 1)

            def place_dst(g, r, v):
                n, blocks, jj = shape_of(g)
                dve.wait_ge(row_in[v], 16 * SUPER * (r + 1))
                dve.tensor_tensor(dst_in_block[:, v % SMALL, 0:blocks], cat[:, v, 0:blocks, P],
                                  block_start[:, bass.ds(first_block(g), blocks)], ALU.subtract).then_inc(dst_counted, 1)

            def make_onehot(g, r, v):
                n, blocks, jj = shape_of(g)
                nodes = node_of if jj == J else short_node_of
                dve.wait_ge(dst_counted, g + 1)
                if after(g, BODY):
                    dve.wait_ge(sum_done, g - BODY + 1)
                for k in range(blocks):
                    last = dve.tensor_scalar(onehot[:, v, k, 0:n * jj], nodes[:, 0:n * jj],
                                             dst_in_block[:, v % SMALL, k:k + 1], None, ALU.is_equal)
                last.then_inc(onehot_ready, 1)

            def less_high_x(g, r, v):
                dve.wait_ge(x_in[v], 16 * (r + 1))
                dve.tensor_tensor(flat_of(x_rest, g, v), flat_of(xs, g, v), upper_half(flat_of(xs, g, v)),
                                  ALU.subtract).then_inc(x_rest_ready, 1)

            def less_middle_x(g, r, v):
                dve.wait_ge(x_rest_ready, g + 1)
                dve.tensor_tensor(flat_of(x_low, g, v), flat_of(x_rest, g, v), upper_half(flat_of(x_rest, g, v)),
                                  ALU.subtract).then_inc(x_split, 1)

            def total_squares(g, r, v):
                n, blocks, jj = shape_of(g)
                t = v % SMALL
                dve.wait_ge(squared, g + 1)
                dve.tensor_reduce(sq_total[0:n, t, 0:blocks * jj], by_node(sq, g, t), AX_X, ALU.add).then_inc(sq_totalled, 1)

            def invert(g, r, v):
                n, blocks, jj = shape_of(g)
                t, m = v % SMALL, blocks * jj
                dve.wait_ge(std_ready, g + 1)
                if after(g, SMALL):
                    dve.wait_ge(normed, g - SMALL + 1)
                dve.reciprocal(rstd[0:n, t, 0:m], std[0:n, t, 0:m]).then_inc(rstd_ready, 1)

            walk(dve, ((6, total_sum), (-1, place_dst), (-1, less_high_x), (6, centre), (-1, less_middle_x),
                       (4, less_high_msg), (-1, make_onehot), (7, invert), (4, less_middle_msg), (6, total_squares)))
            dve.wait_ge(general_done, 1)
            needed = dve.value_load(general[0:1, 0:1], min_val=0, max_val=1)
            with dve.If(needed > 0):
                general_engine["vector"](dve)


_INS = ['x', 'src', 'dst', 'edge_attr_32', 'L0_gnn_W1', 'L0_gnn_b1', 'L0_gnn_W2', 'L0_gnn_b2']


def kernel(**inputs):
    import numpy as _np
    import concourse.bacc as _bacc
    from concourse import mybir as _mybir
    from concourse.bass_utils import run_bass_kernel_spmd as _run

    nc = _bacc.Bacc("TRN2", target_bir_lowering=False, num_devices=1)
    arrays, args = {}, []
    for name in _INS:
        a = _np.ascontiguousarray(inputs[name])
        arrays[f"in_{name}_dram"] = a
        args.append(nc.dram_tensor(f"in_{name}_dram", a.shape, _mybir.dt.from_np(a.dtype), kind="ExternalInput").ap())
    shape = _np.asarray(inputs['x']).shape
    args.append(nc.dram_tensor("out_0_dram", shape, _mybir.dt.float32, kind="ExternalOutput").ap())
    gnn_resnorm_kernel(nc, *args)
    r = _run(nc, [arrays], core_ids=[0])
    return r.results[0]["out_0_dram"]
```
